# Optimizing a Trainium2 kernel written in Bass

```python
import numpy as np
import jax
import jax.numpy as jnp

def _softmax(x, axis=-1):
    return jax.nn.softmax(x, axis=axis)

def _gelu(x):
    return jax.nn.gelu(x, approximate=True)

def _silu(x):
    return jax.nn.silu(x)

def _sigmoid(x):
    return jax.nn.sigmoid(x)

def _layernorm(x, axis=-1, eps=1e-05):
    m = jnp.mean(x, axis=axis, keepdims=True)
    v = jnp.var(x, axis=axis, keepdims=True)
    return (x - m) / jnp.sqrt(v + eps)

def _scatter_add(tgt, idx, src, axis=0):
    return tgt.at[idx].add(src)

def _segment_sum(src, seg, n):
    return jax.ops.segment_sum(src, seg, n)
kernel_name = 'mk_gnn_resnorm_d4_gnn_r32_6d5489'

def setup_inputs(seed: int=0):
    np.random.seed(seed)
    _w = jnp.asarray

    def _rec_inputs():
        import jax
        import jax.numpy as jnp
        _gk = jax.random.key(seed)
        x = -0.0002117 + 1 * jax.random.normal(jax.random.fold_in(_gk, 1), (50000, 256), jnp.float32)
        src = jax.random.randint(jax.random.fold_in(_gk, 2), (50000,), 0, 50000, jnp.int32)
        dst = jnp.minimum((50000 * jax.random.uniform(jax.random.fold_in(_gk, 3), (50000,)) ** 2.0).astype(jnp.int32), 49999)
        _o = jnp.argsort(dst, stable=True)
        src = src[_o]
        dst = dst[_o]
        edge_weight = jax.random.uniform(jax.random.fold_in(_gk, 14), (50000,), jnp.float32, 0.0, 1)
        return (x, src, dst, edge_weight)
    x, src, dst, edge_weight = _rec_inputs()

    def _L0_gnn_setup():
        import jax, jax.numpy as jnp
        import numpy as np
        BN_EPS = 1e-05

        def _batchnorm(h, gamma, beta):
            mean = jnp.mean(h, axis=0, keepdims=True)
            var = jnp.var(h, axis=0, keepdims=True)
            return (h - mean) * jax.lax.rsqrt(var + BN_EPS) * gamma + beta
        key = jax.random.key(seed)
        ks = jax.random.split(key, 10)
        N, E, D = (3125, 100000, 256)
        x = jax.random.normal(ks[0], (N, D), dtype=jnp.float32)
        edge_src = jax.random.randint(ks[1], (E,), 0, N, dtype=jnp.int32)
        edge_dst = jax.random.randint(ks[2], (E,), 0, N, dtype=jnp.int32)
        edge_vals = jnp.ones((E,), dtype=jnp.float32)
        n_norm = jax.random.uniform(ks[3], (N, 1), dtype=jnp.float32)
        s = 1.0 / np.sqrt(D)
        w1 = jax.random.uniform(ks[4], (D, D), jnp.float32, -s, s)
        gamma1 = jnp.ones((D,), jnp.float32)
        beta1 = jnp.zeros((D,), jnp.float32)
        w2 = jax.random.uniform(ks[5], (D, D), jnp.float32, -s, s)
        eps_weight = jnp.zeros((1,), jnp.float32)
        gamma_h = jnp.ones((D,), jnp.float32)
        beta_h = jnp.zeros((D,), jnp.float32)
        return {'x': x, 'edge_src': edge_src, 'edge_dst': edge_dst, 'edge_vals': edge_vals, 'n_norm': n_norm, 'w1': w1, 'gamma1': gamma1, 'beta1': beta1, 'w2': w2, 'eps_weight': eps_weight, 'gamma_h': gamma_h, 'beta_h': beta_h}
    _L0_gnn_all = _L0_gnn_setup()
    _L0_gnn_in = {k: v for k, v in _L0_gnn_all.items() if k in ('w1', 'gamma1', 'beta1', 'w2', 'eps_weight', 'gamma_h', 'beta_h')}
    del _L0_gnn_all

    def _L1_gnn_setup():
        import jax, jax.numpy as jnp
        import numpy as np
        from jax.ops import segment_sum, segment_max
        N_NODES = 50000
        N_EDGES = 25000
        IN_DIM = 256
        OUT_DIM = 64
        N_HEADS = 4
        key = jax.random.key(seed)
        k1, k2, k3, k4, k5, k6 = jax.random.split(key, 6)
        h = jax.random.normal(k1, (N_NODES, IN_DIM), dtype=jnp.float32)
        src = jax.random.randint(k2, (N_EDGES,), 0, N_NODES, dtype=jnp.int32)
        dst = jax.random.randint(k3, (N_EDGES,), 0, N_NODES, dtype=jnp.int32)
        W = jax.random.normal(k4, (N_HEADS, IN_DIM, OUT_DIM), dtype=jnp.float32) * 0.05
        a_src = jax.random.normal(k5, (N_HEADS, OUT_DIM), dtype=jnp.float32) * 0.05
        a_dst = jax.random.normal(k6, (N_HEADS, OUT_DIM), dtype=jnp.float32) * 0.05
        return {'h': h, 'src': src, 'dst': dst, 'W': W, 'a_src': a_src, 'a_dst': a_dst}
    _L1_gnn_all = _L1_gnn_setup()
    _L1_gnn_in = {k: v for k, v in _L1_gnn_all.items() if k in ('W', 'a_src', 'a_dst')}
    del _L1_gnn_all

    def _L2_gnn_setup():
        import jax, jax.numpy as jnp
        import numpy as np
        N_NODES = 50000
        N_EDGES = 25000
        D_IN = 256
        D_OUT = 256
        BN_EPS = 1e-05

        def _forward(x, edge_index, w1, b1, gamma, beta, w2, b2, w_gcn, b_gcn):
            n = x.shape[0]
            h = x @ w1.T + b1
            mean = jnp.mean(h, axis=0)
            var = jnp.var(h, axis=0)
            h = (h - mean) * jax.lax.rsqrt(var + BN_EPS) * gamma + beta
            h = jax.nn.relu(h)
            h = h @ w2.T + b2
            xw = h @ w_gcn.T
            src = jnp.concatenate([edge_index[0], jnp.arange(n, dtype=edge_index.dtype)])
            dst = jnp.concatenate([edge_index[1], jnp.arange(n, dtype=edge_index.dtype)])
            deg = jax.ops.segment_sum(jnp.ones_like(dst, dtype=xw.dtype), dst, num_segments=n)
            dinv = jnp.where(deg > 0, jax.lax.rsqrt(jnp.maximum(deg, 1.0)), 0.0)
            norm = dinv[src] * dinv[dst]
            msgs = xw[src] * norm[:, None]
            out = jax.ops.segment_sum(msgs, dst, num_segments=n) + b_gcn
            return out
        key = jax.random.key(seed)
        ks = jax.random.split(key, 8)
        x = jax.random.normal(ks[0], (N_NODES, D_IN), dtype=jnp.float32)
        edge_index = jax.random.randint(ks[1], (2, N_EDGES), 0, N_NODES, dtype=jnp.int64)
        s1 = 1.0 / np.sqrt(D_IN)
        s2 = 1.0 / np.sqrt(D_OUT)
        w1 = jax.random.uniform(ks[2], (D_OUT, D_IN), jnp.float32, -s1, s1)
        b1 = jax.random.uniform(ks[3], (D_OUT,), jnp.float32, -s1, s1)
        gamma = jnp.ones((D_OUT,), jnp.float32)
        beta = jnp.zeros((D_OUT,), jnp.float32)
        w2 = jax.random.uniform(ks[4], (D_OUT, D_OUT), jnp.float32, -s2, s2)
        b2 = jax.random.uniform(ks[5], (D_OUT,), jnp.float32, -s2, s2)
        w_gcn = jax.random.uniform(ks[6], (D_OUT, D_OUT), jnp.float32, -s2, s2)
        b_gcn = jnp.zeros((D_OUT,), jnp.float32)
        return {'x': x, 'edge_index': edge_index, 'w1': w1, 'b1': b1, 'gamma': gamma, 'beta': beta, 'w2': w2, 'b2': b2, 'w_gcn': w_gcn, 'b_gcn': b_gcn}
    _L2_gnn_all = _L2_gnn_setup()
    _L2_gnn_in = {k: v for k, v in _L2_gnn_all.items() if k in ('w1', 'b1', 'gamma', 'beta', 'w2', 'b2', 'w_gcn', 'b_gcn')}
    del _L2_gnn_all

    def _L3_gnn_setup():
        import jax, jax.numpy as jnp
        import numpy as np
        N = 3125
        E = 50000
        IN_FEATS = 256
        OUT_FEATS = 256
        MAXK = 32

        def _maxk(x, k):
            _, idx = jax.lax.top_k(x, k)
            rows = jnp.arange(x.shape[0])[:, None]
            mask = jnp.zeros_like(x).at[rows, idx].set(1.0)
            return x * mask
        key = jax.random.key(seed)
        k1, k2, k3, k4, k5 = jax.random.split(key, 5)
        feat = jax.random.normal(k1, (N, IN_FEATS), dtype=jnp.float32)
        W_self = jax.random.normal(k2, (IN_FEATS, OUT_FEATS), dtype=jnp.float32) * (1.0 / np.sqrt(IN_FEATS))
        W_neigh = jax.random.normal(k3, (IN_FEATS, OUT_FEATS), dtype=jnp.float32) * (1.0 / np.sqrt(IN_FEATS))
        src = jax.random.randint(k4, (E,), 0, N, dtype=jnp.int64)
        dst = jax.random.randint(k5, (E,), 0, N, dtype=jnp.int64)
        return {'feat': feat, 'W_self': W_self, 'W_neigh': W_neigh, 'src': src, 'dst': dst}
    _L3_gnn_all = _L3_gnn_setup()
    _L3_gnn_in = {k: v for k, v in _L3_gnn_all.items() if k in ('W_self', 'W_neigh')}
    del _L3_gnn_all
    return {'x': x, 'src': src, 'dst': dst, 'edge_weight': edge_weight, 'L0_gnn_w1': _L0_gnn_in['w1'], 'L0_gnn_gamma1': _L0_gnn_in['gamma1'], 'L0_gnn_beta1': _L0_gnn_in['beta1'], 'L0_gnn_w2': _L0_gnn_in['w2'], 'L0_gnn_eps_weight': _L0_gnn_in['eps_weight'], 'L0_gnn_gamma_h': _L0_gnn_in['gamma_h'], 'L0_gnn_beta_h': _L0_gnn_in['beta_h'], 'L1_gnn_W': _L1_gnn_in['W'], 'L1_gnn_a_src': _L1_gnn_in['a_src'], 'L1_gnn_a_dst': _L1_gnn_in['a_dst'], 'L2_gnn_w1': _L2_gnn_in['w1'], 'L2_gnn_b1': _L2_gnn_in['b1'], 'L2_gnn_gamma': _L2_gnn_in['gamma'], 'L2_gnn_beta': _L2_gnn_in['beta'], 'L2_gnn_w2': _L2_gnn_in['w2'], 'L2_gnn_b2': _L2_gnn_in['b2'], 'L2_gnn_w_gcn': _L2_gnn_in['w_gcn'], 'L2_gnn_b_gcn': _L2_gnn_in['b_gcn'], 'L3_gnn_W_self': _L3_gnn_in['W_self'], 'L3_gnn_W_neigh': _L3_gnn_in['W_neigh']}

def reference(x, src, dst, edge_weight, L0_gnn_w1, L0_gnn_gamma1, L0_gnn_beta1, L0_gnn_w2, L0_gnn_eps_weight, L0_gnn_gamma_h, L0_gnn_beta_h, L1_gnn_W, L1_gnn_a_src, L1_gnn_a_dst, L2_gnn_w1, L2_gnn_b1, L2_gnn_gamma, L2_gnn_beta, L2_gnn_w2, L2_gnn_b2, L2_gnn_w_gcn, L2_gnn_b_gcn, L3_gnn_W_self, L3_gnn_W_neigh):
    import jax
    import jax.numpy as jnp

    def _L0_gnn_ref(x, edge_src, edge_dst, edge_vals, n_norm, w1, gamma1, beta1, w2, eps_weight, gamma_h, beta_h):
        import jax, jax.numpy as jnp
        import numpy as np
        BN_EPS = 1e-05

        def _batchnorm(h, gamma, beta):
            mean = jnp.mean(h, axis=0, keepdims=True)
            var = jnp.var(h, axis=0, keepdims=True)
            return (h - mean) * jax.lax.rsqrt(var + BN_EPS) * gamma + beta
        N = x.shape[0]
        msgs = edge_vals[:, None] * x[edge_src]
        agg = jax.ops.segment_sum(msgs, edge_dst, num_segments=N)
        y = agg + eps_weight * x
        h = jax.nn.relu(_batchnorm(y @ w1.T, gamma1, beta1))
        y = h @ w2.T
        y = y * n_norm
        y = _batchnorm(y, gamma_h, beta_h)
        y = jax.nn.relu(y)
        y = y + x
        return y

    def _L1_gnn_ref(h, src, dst, W, a_src, a_dst):
        import jax, jax.numpy as jnp
        import numpy as np
        from jax.ops import segment_sum, segment_max
        N_NODES = 50000
        N_EDGES = 25000
        IN_DIM = 256
        OUT_DIM = 64
        N_HEADS = 4
        n = h.shape[0]
        z = jnp.einsum('ni,hio->nho', h, W)
        e_src = jnp.einsum('nho,ho->nh', z, a_src)
        e_dst = jnp.einsum('nho,ho->nh', z, a_dst)
        e = jax.nn.leaky_relu(e_src[src] + e_dst[dst], negative_slope=0.01)
        m = segment_max(e, dst, num_segments=n)
        e_exp = jnp.exp(e - m[dst])
        denom = segment_sum(e_exp, dst, num_segments=n)
        alpha = e_exp / denom[dst]
        msg = alpha[:, :, None] * z[src]
        out = segment_sum(msg, dst, num_segments=n)
        return out.reshape(n, N_HEADS * OUT_DIM)

    def _L2_gnn_ref(x, edge_index, w1, b1, gamma, beta, w2, b2, w_gcn, b_gcn):
        import jax, jax.numpy as jnp
        import numpy as np
        N_NODES = 50000
        N_EDGES = 25000
        D_IN = 256
        D_OUT = 256
        BN_EPS = 1e-05

        def _forward(x, edge_index, w1, b1, gamma, beta, w2, b2, w_gcn, b_gcn):
            n = x.shape[0]
            h = x @ w1.T + b1
            mean = jnp.mean(h, axis=0)
            var = jnp.var(h, axis=0)
            h = (h - mean) * jax.lax.rsqrt(var + BN_EPS) * gamma + beta
            h = jax.nn.relu(h)
            h = h @ w2.T + b2
            xw = h @ w_gcn.T
            src = jnp.concatenate([edge_index[0], jnp.arange(n, dtype=edge_index.dtype)])
            dst = jnp.concatenate([edge_index[1], jnp.arange(n, dtype=edge_index.dtype)])
            deg = jax.ops.segment_sum(jnp.ones_like(dst, dtype=xw.dtype), dst, num_segments=n)
            dinv = jnp.where(deg > 0, jax.lax.rsqrt(jnp.maximum(deg, 1.0)), 0.0)
            norm = dinv[src] * dinv[dst]
            msgs = xw[src] * norm[:, None]
            out = jax.ops.segment_sum(msgs, dst, num_segments=n) + b_gcn
            return out
        return _forward(x, edge_index, w1, b1, gamma, beta, w2, b2, w_gcn, b_gcn)

    def _L3_gnn_ref(feat, W_self, W_neigh, src, dst):
        import jax, jax.numpy as jnp
        import numpy as np
        N = 3125
        E = 50000
        IN_FEATS = 256
        OUT_FEATS = 256
        MAXK = 32

        def _maxk(x, k):
            _, idx = jax.lax.top_k(x, k)
            rows = jnp.arange(x.shape[0])[:, None]
            mask = jnp.zeros_like(x).at[rows, idx].set(1.0)
            return x * mask
        n = feat.shape[0]
        h_self = feat @ W_self
        h_neigh = feat @ W_neigh
        h_sparse = _maxk(h_neigh, MAXK)
        msg = h_sparse[src]
        summed = jax.ops.segment_sum(msg, dst, num_segments=n)
        deg = jax.ops.segment_sum(jnp.ones((src.shape[0],), dtype=feat.dtype), dst, num_segments=n)
        neigh = summed / jnp.maximum(deg, 1.0)[:, None]
        return h_self + neigh
    edge_index = jnp.stack([src, dst])
    deg = jnp.maximum(jax.ops.segment_sum(jnp.ones(dst.shape, jnp.float32), dst, num_segments=50000), 1.0)
    deg_isqrt = deg ** (-0.5)
    x = _layernorm(x + _L0_gnn_ref(x, src, dst, edge_weight, deg_isqrt[:, None], L0_gnn_w1, L0_gnn_gamma1, L0_gnn_beta1, L0_gnn_w2, L0_gnn_eps_weight, L0_gnn_gamma_h, L0_gnn_beta_h), axis=-1)
    x = _layernorm(x + _L1_gnn_ref(x, src, dst, L1_gnn_W, L1_gnn_a_src, L1_gnn_a_dst), axis=-1)
    x = _layernorm(x + _L2_gnn_ref(x, edge_index, L2_gnn_w1, L2_gnn_b1, L2_gnn_gamma, L2_gnn_beta, L2_gnn_w2, L2_gnn_b2, L2_gnn_w_gcn, L2_gnn_b_gcn), axis=-1)
    x = _layernorm(x + _L3_gnn_ref(x, L3_gnn_W_self, L3_gnn_W_neigh, src, dst), axis=-1)
    return x

_drawn_inputs = setup_inputs


def setup_inputs(seed=0):
    import zlib

    import numpy as np

    out = dict(_drawn_inputs(seed))
    spreads = {'L0_gnn_gamma1': (1.0, 0.2),
     'L0_gnn_beta1': (0.0, 0.1),
     'L0_gnn_gamma_h': (1.0, 0.2),
     'L0_gnn_beta_h': (0.0, 0.1),
     'L2_gnn_gamma': (1.0, 0.2),
     'L2_gnn_beta': (0.0, 0.1),
     'L2_gnn_b_gcn': (0.0, 0.1)}
    factors = {}
    for name, (base, spread) in spreads.items():
        noise = np.random.default_rng([zlib.crc32(name.encode()), seed]).standard_normal(out[name].shape)
        drawn = base * np.exp(spread * noise) if base else spread * noise
        out[name] = jnp.asarray(drawn.astype(out[name].dtype))
    for name, factor in factors.items():
        out[name] = (out[name] * factor).astype(out[name].dtype)
    return out
```

```python
import concourse.bass as bass
from concourse import mybir
from contextlib import ExitStack

F32 = mybir.dt.float32
BF16 = mybir.dt.bfloat16
F16 = mybir.dt.float16
I32 = mybir.dt.int32
ALU = mybir.AluOpType
ACT = mybir.ActivationFunctionType
AX = mybir.AxisListType

P = 128
N = 50000
E = 50000
D = 256
H = 4
HD = D // H
KC = D // P
TOPK = 32
EPS = 1e-5
BIG = 1e30
TAKEN = -3.0e38

EC = -(-E // P)
EB = 17
ESTEPS = EC // EB
assert EC == EB * ESTEPS
LASTP = E - (P - 1) * EC
SUBS = [(0, 5), (5, 9), (9, 13), (13, 17)]
ZERO_ROW = P * EC

NT = -(-N // P)
G = 3
GN = G * P
GROUPS = N // GN
TAILN = N - GROUPS * GN
PAIRS = GROUPS // 2
assert GROUPS == 2 * PAIRS and TAILN <= P and NT == GROUPS * G + 1
NPAD = NT * P


class Step:

    def __init__(self, g, par, use, tiles=G, rows=P):
        self.g, self.par, self.use, self.tiles, self.rows = g, par, use, tiles, rows
        self.first = isinstance(use, int) and use == 0
        self.n = rows if tiles == 1 else tiles * rows


def done(use, per=1):
    return (use + 1) * per


def node_pass(eng, *stages):
    most = max(s for s, _ in stages)
    peel = 1 + (most + 1) // 2
    for g in range(2 * peel):
        for s, body in stages:
            if g >= s:
                body(Step(g - s, (g - s) % 2, (g - s) // 2))
    with eng.Fori(peel, PAIRS) as i:
        for q in range(2):
            for s, body in stages:
                par = (q - s) % 2
                back = (q - s - par) // 2
                body(Step(2 * i + (q - s), par, i + back))
    for g in range(GROUPS, GROUPS + most + 1):
        for s, body in stages:
            if g - s < GROUPS:
                body(Step(g - s, (g - s) % 2, (g - s) // 2))
            elif g - s == GROUPS:
                body(Step(GROUPS, 0, PAIRS, 1, TAILN))


def build(nc, io, out):
    top = ExitStack()
    with top:
        def keep(name, shape, dt=F32):
            return top.enter_context(nc.sbuf_tensor(name, shape, dt))

        def dram(name, shape, dt=F32):
            return nc.dram_tensor(name, shape, dt, kind="Internal").ap()

        opened = []

        def signal(name):
            opened.append(nc.alloc_semaphore(name))
            return opened[-1]

        def close_phase():
            nc.clear_and_free_semaphores(opened)
            opened.clear()
            nc.all_engine_barrier()

        tot = dram("tot", [P * EC + P, D])
        hT = dram("hT", [GROUPS + 1, P, KC * GN])
        x1d = dram("x1d", [N, D])
        x2d = dram("x2d", [N, D])
        zd = dram("zd", [N, D])
        based = dram("based", [N, D])
        esd = dram("esd", [P * NT, 2 * H])
        nnd = dram("nnd", [NT, P])

        src_i = keep("src_i", [P, EC + EB], I32)
        ssc_i = keep("ssc_i", [P, EC + EB], I32)
        dsc_i = keep("dsc_i", [P, EC + EB], I32)
        nlast = keep("nlast", [P, NT], I32)
        fix_i = keep("fix_i", [P, 1], I32)
        same = keep("same", [P, EC])
        wgt = keep("wgt", [P, EC])
        alpha = keep("alpha", [P, H, EC])
        nnorm = keep("nnorm", [P, NT])
        dinv = keep("dinv", [P, NT])
        rdeg = keep("rdeg", [P, NT])
        carryT = keep("carryT", [P, P])
        fl4 = keep("fl4", [P, 4, P])
        firstrun = keep("firstrun", [P, EC])
        lastrun = keep("lastrun", [P, EC])
        midrun = keep("midrun", [P, EC])
        ident = keep("ident", [P, P])
        ones = keep("ones", [P, P])
        bn = keep("bn", [P, 3, 2, KC])
        scores = keep("scores", [P, NT, 2 * H])

        with ExitStack() as c:
            def sb(name, shape, dt=F32):
                return c.enter_context(nc.sbuf_tensor(name, shape, dt))

            def sem(name):
                return signal(name)

            dst_i = sb("dst_i", [P, EC], I32)
            dst_f = sb("dst_f", [P, EC])
            t_i = sb("t_i", [P, EC], I32)
            dhi = sb("dhi", [P, EC])
            dlo = sb("dlo", [P, EC])
            t_f = sb("t_f", [P, EC])
            iota_hi = sb("iota_hi", [P, NT], F16)
            iota_lo = sb("iota_lo", [P, P], F16)
            iota_p = sb("iota_p", [P, 1])
            iota_pe = sb("iota_pe", [P, 1])
            upper = sb("upper", [P, P])
            zrow = sb("zrow", [P, D])
            zb = sb("zb", [P, P], BF16)
            zh = sb("zh", [P, NT], BF16)
            one_hi = sb("one_hi", [P, EB, NT], BF16)
            one_lo = sb("one_lo", [P, EB, P], BF16)
            deg = sb("deg", [P, NT])
            nxt = sb("nxt", [P, EC])
            zec = sb("zec", [P, EC])
            sq = sb("sq", [P, 3, NT])
            runlen = sb("runlen", [P, 2])
            diag = sb("diag", [P, 3, P])
            whole = sb("whole", [P, 1])
            nnT = sb("nnT", [P, 4, P])
            hist = c.enter_context(nc.psum_tensor("hist", [P, 512], F32))
            cum = c.enter_context(nc.psum_tensor("cum", [P, 512], F32))
            colsum = c.enter_context(nc.psum_tensor("colsum", [P, 512], F32))
            rows = c.enter_context(nc.psum_tensor("rows", [P, 512], F32))
            nnps = c.enter_context(nc.psum_tensor("nnps", [P, 512], F32))

            s_ld = sem("s_ld")
            s_zr = sem("s_zr")
            s_set = sem("s_set")
            s_io = sem("s_io")
            s_v = sem("s_v")
            s_oh = sem("s_oh")
            s_mm = sem("s_mm")
            s_hist = sem("s_hist")
            s_deg = sem("s_deg")
            s_cum = sem("s_cum")
            s_sq = sem("s_sq")
            s_sqv = sem("s_sqv")
            s_diag = sem("s_diag")
            s_rows = sem("s_rows")
            s_nn = sem("s_nn")
            s_nnT = sem("s_nnT")
            s_nnc = sem("s_nnc")
            s_st = sem("s_st")
            block = c.enter_context(nc.Block())

            def edges(flat):
                main = flat[0:112 * EC].rearrange("(p t) -> p t", t=EC)
                rest = flat[112 * EC:(P - 1) * EC].rearrange("(p t) -> p t", t=EC)
                last = flat[(P - 1) * EC:E].rearrange("(p t) -> p t", p=1)
                return [(slice(0, 112), EC, main), (slice(112, P - 1), EC, rest), (slice(P - 1, P), LASTP, last)]

            @block.sync
            def _(sp):
                sp.wait_ge(s_set, 3)
                for tile, flat in ((src_i, io["src"]), (dst_i, io["dst"]), (wgt, io["edge_weight"])):
                    for ps, cols, part in edges(flat):
                        sp.dma_start(tile[ps, 0:cols], part).then_inc(s_ld, 16)
                sp.wait_ge(s_set, 4)
                sp.dma_start(tot[ZERO_ROW:ZERO_ROW + P, :], zrow[:, :]).then_inc(s_zr, 16)
                sp.wait_ge(s_nnc, 4)
                for b in range(4):
                    r = min(P, NT - b * P)
                    sp.dma_start(nnd[b * P:b * P + r, :], nnT[0:r, b, :]).then_inc(s_st, 16)
                sp.wait_ge(s_zr, 16)
                sp.wait_ge(s_st, 64)

            @block.gpsimd
            def _(pool):
                pool.iota(iota_hi[:, :], pattern=[[1, NT]], base=0, channel_multiplier=0,
                          allow_small_or_imprecise_dtypes=True).then_inc(s_io, 1)
                pool.iota(iota_lo[:, :], pattern=[[1, P]], base=0, channel_multiplier=0,
                          allow_small_or_imprecise_dtypes=True).then_inc(s_io, 1)
                pool.iota(iota_p[:, :], pattern=[[0, 1]], base=0, channel_multiplier=1,
                          allow_small_or_imprecise_dtypes=True).then_inc(s_io, 1)
                pool.iota(iota_pe[:, :], pattern=[[0, 1]], base=0, channel_multiplier=EC,
                          allow_small_or_imprecise_dtypes=True).then_inc(s_io, 1)

            @block.scalar
            def _(act):
                act.wait_ge(s_sqv, 1)
                nc.scalar.activation(sq[:, :, :], sq[:, :, :], ACT.Sqrt).then_inc(s_sq, 1)
                for b in range(4):
                    r = min(P, NT - b * P)
                    if b == 0:
                        act.wait_ge(s_nnT, 4)
                    nc.scalar.copy(nnT[0:r, b, :], nnps[0:r, b * P:(b + 1) * P]).then_inc(s_nnc, 1)

            @block.tensor
            def _(pe):
                pe.wait_ge(s_set, 6)
                nc.tensor.matmul(hist[:, 0:NT], zb[:, :], zh[:, :], start=True, stop=False)
                with pe.Fori(0, ESTEPS) as i:
                    for b in range(EB):
                        pe.wait_ge(s_oh, i * EB + (b + 1))
                        nc.tensor.matmul(hist[:, 0:NT], one_lo[:, b, :], one_hi[:, b, :], start=False,
                                         stop=False).then_inc(s_mm, 1)
                nc.tensor.matmul(hist[:, 0:NT], zb[:, :], zh[:, :], start=False, stop=True).then_inc(s_hist, 1)
                pe.wait_ge(s_deg, 1)
                nc.tensor.matmul(cum[:, 0:NT], upper[:, :], deg[:, :], start=True, stop=True).then_inc(s_cum, 1)
                nc.tensor.matmul(colsum[:, 0:NT], ones[:, :], deg[:, :], start=True, stop=True).then_inc(s_cum, 1)
                pe.wait_ge(s_diag, 1)
                nc.tensor.matmul(rows[:, 0:3 * P], ones[:, :], diag[:, :, :].rearrange("p a b -> p (a b)"),
                                 start=True, stop=True).then_inc(s_rows, 1)
                pe.wait_ge(s_nn, 1)
                for b in range(4):
                    r = min(P, NT - b * P)
                    nc.tensor.transpose(nnps[0:r, b * P:(b + 1) * P], nnorm[:, b * P:b * P + r],
                                        ident[:, :]).then_inc(s_nnT, 1)

            @block.vector
            def _(dve):
                n = [0]

                def link(ins):
                    n[0] += 1
                    ins.then_inc(s_v, 1)
                    dve.wait_ge(s_v, n[0])

                v = nc.vector
                v.memset(src_i[:, :], 0).then_inc(s_set, 1)
                v.memset(dst_i[:, :], N).then_inc(s_set, 1)
                v.memset(wgt[:, :], 0.0).then_inc(s_set, 1)
                v.memset(zrow[:, :], 0.0).then_inc(s_set, 1)
                v.memset(zb[:, :], 0.0).then_inc(s_set, 1)
                v.memset(zh[:, :], 0.0).then_inc(s_set, 1)
                v.memset(ones[:, :], 1.0)
                v.memset(zec[:, :], 0.0)
                link(v.memset(same[:, :], 0.0))
                dve.wait_ge(s_io, 4)
                link(v.tensor_scalar(upper[:, :], iota_lo[:, :], iota_p[:, 0:1], None, ALU.is_ge))
                link(v.tensor_scalar(ident[:, :], iota_lo[:, :], iota_p[:, 0:1], None, ALU.is_equal))
                dve.wait_ge(s_ld, 9 * 16)
                link(v.tensor_copy(dst_f[:, :], dst_i[:, :]))
                link(v.tensor_scalar(t_i[:, :], dst_i[:, :], 7, None, ALU.logical_shift_right))
                link(v.tensor_copy(dhi[:, :], t_i[:, :]))
                link(v.tensor_scalar(t_i[:, :], dst_i[:, :], P - 1, None, ALU.bitwise_and))
                link(v.tensor_copy(dlo[:, :], t_i[:, :]))

                def one_hot(i, b, first):
                    if not first:
                        dve.wait_ge(s_mm, (i - 1) * EB + (b + 1))
                    v.tensor_scalar(one_hi[:, b, :], iota_hi[:, :], dhi[:, bass.ds(i * EB + b, 1)], None,
                                    ALU.is_equal)
                    v.tensor_scalar(one_lo[:, b, :], iota_lo[:, :], dlo[:, bass.ds(i * EB + b, 1)], None,
                                    ALU.is_equal).then_inc(s_oh, 1)

                for b in range(EB):
                    one_hot(0, b, True)
                with dve.Fori(1, ESTEPS) as i:
                    for b in range(EB):
                        one_hot(i, b, False)

                v.memset(ssc_i[:, :], 0)
                link(v.memset(dsc_i[:, :], 0))
                link(v.scalar_tensor_tensor(dsc_i[:, 0:EC], dlo[:, :], float(NT), dhi[:, :], ALU.mult, ALU.add))
                link(v.tensor_scalar(t_i[:, :], src_i[:, 0:EC], 7, None, ALU.logical_shift_right))
                link(v.tensor_copy(dhi[:, :], t_i[:, :]))
                link(v.tensor_scalar(t_i[:, :], src_i[:, 0:EC], P - 1, None, ALU.bitwise_and))
                link(v.tensor_copy(dlo[:, :], t_i[:, :]))
                link(v.scalar_tensor_tensor(ssc_i[:, 0:EC], dlo[:, :], float(NT), dhi[:, :], ALU.mult, ALU.add))

                link(v.tensor_tensor(same[:, 1:EC], dst_f[:, 1:EC], dst_f[:, 0:EC - 1], ALU.is_equal))
                link(v.memset(nxt[:, :], 0.0))
                link(v.tensor_copy(nxt[:, 0:EC - 1], same[:, 1:EC]))
                link(v.tensor_copy(t_f[:, :], same[:, :]))
                link(v.memset(t_f[:, 0:1], 1.0))
                link(v.tensor_tensor_scan(firstrun[:, :], t_f[:, :], zec[:, :], 1.0, ALU.mult, ALU.add))
                link(v.tensor_copy(t_f[:, :], nxt[:, :]))
                link(v.memset(t_f[:, EC - 1:EC], 1.0))
                link(v.tensor_tensor_scan(lastrun[:, ::-1], t_f[:, ::-1], zec[:, :], 1.0, ALU.mult, ALU.add))
                link(v.tensor_reduce(runlen[:, 0:1], firstrun[:, :], AX.X, ALU.add))
                link(v.tensor_scalar(runlen[:, 0:1], runlen[:, 0:1], -1.0, None, ALU.add))
                link(v.tensor_tensor(runlen[:, 1:2], runlen[:, 0:1], iota_pe[:, :], ALU.add))
                link(v.tensor_copy(fix_i[:, :], runlen[:, 1:2]))
                link(v.tensor_copy(whole[:, :], firstrun[:, EC - 1:EC]))
                link(v.tensor_scalar(t_f[:, :], firstrun[:, :], -1.0, 1.0, ALU.mult, ALU.add))
                link(v.tensor_tensor(lastrun[:, :], lastrun[:, :], t_f[:, :], ALU.mult))
                link(v.tensor_tensor(midrun[:, :], t_f[:, :], lastrun[:, :], ALU.subtract))

                dve.wait_ge(s_hist, 1)
                v.tensor_copy(deg[:, :], hist[:, 0:NT]).then_inc(s_deg, 1)
                v.tensor_scalar(diag[:, 0, :], ident[:, :], dst_f[:, 0:1], None, ALU.mult)
                v.tensor_scalar(diag[:, 1, :], ident[:, :], dst_f[:, EC - 1:EC], None, ALU.mult)
                v.tensor_scalar(diag[:, 2, :], ident[:, :], whole[:, 0:1], None, ALU.mult).then_inc(s_diag, 1)
                dve.wait_ge(s_rows, 1)
                link(v.tensor_scalar(fl4[:, 0, :], rows[:, P:2 * P], dst_f[:, 0:1], None, ALU.is_equal))
                link(v.tensor_scalar(fl4[:, 1, :], rows[:, 0:P], dst_f[:, 0:1], None, ALU.is_equal))
                link(v.tensor_scalar(fl4[:, 2, :], rows[:, P:2 * P], dst_f[:, EC - 1:EC], None, ALU.is_equal))
                link(v.tensor_scalar(fl4[:, 3, :], rows[:, 0:P], dst_f[:, EC - 1:EC], None, ALU.is_equal))
                link(v.tensor_scalar(diag[:, 2, :], rows[:, 2 * P:3 * P], -1.0, 1.0, ALU.mult, ALU.add))
                link(v.tensor_tensor(fl4[:, 1, :], fl4[:, 1, :], diag[:, 2, :], ALU.mult))
                link(v.tensor_tensor(fl4[:, 3, :], fl4[:, 3, :], diag[:, 2, :], ALU.mult))
                link(v.tensor_scalar(carryT[:, :], rows[:, 0:P], dst_f[:, EC - 1:EC], None, ALU.is_equal))
                link(v.tensor_tensor(diag[:, 0, :], upper[:, :], ident[:, :], ALU.subtract))
                link(v.tensor_tensor(carryT[:, :], carryT[:, :], diag[:, 0, :], ALU.mult))

                dve.wait_ge(s_cum, 2)
                link(v.tensor_copy(dst_f[:, 0:NT], colsum[:, 0:NT]))
                link(v.tensor_tensor_scan(t_f[:, 0:NT], dst_f[:, 0:NT], zec[:, 0:NT], 0.0, ALU.add, ALU.add))
                link(v.tensor_tensor(t_f[:, 0:NT], t_f[:, 0:NT], dst_f[:, 0:NT], ALU.subtract))
                link(v.tensor_tensor(t_f[:, 0:NT], t_f[:, 0:NT], cum[:, 0:NT], ALU.add))
                link(v.tensor_scalar(t_f[:, 0:NT], t_f[:, 0:NT], -1.0 - ZERO_ROW, None, ALU.add))
                link(v.scalar_tensor_tensor(t_f[:, 0:NT], deg[:, :], 0.0, t_f[:, 0:NT], ALU.is_gt, ALU.mult))
                link(v.tensor_scalar(t_f[:, 0:NT], t_f[:, 0:NT], float(ZERO_ROW), None, ALU.add))
                link(v.tensor_copy(nlast[:, :], t_f[:, 0:NT]))
                link(v.tensor_scalar(sq[:, 0, :], deg[:, :], 1.0, None, ALU.max))
                link(v.tensor_scalar(sq[:, 1, :], deg[:, :], 1.0, None, ALU.add))
                link(v.reciprocal(rdeg[:, :], sq[:, 0, :]))
                v.memset(sq[:, 2, :], 1.0).then_inc(s_sqv, 1)
                dve.wait_ge(s_sq, 1)
                link(v.reciprocal(dinv[:, :], sq[:, 1, :]))
                v.reciprocal(nnorm[:, :], sq[:, 0, :]).then_inc(s_nn, 1)

        close_phase()

        def edge_pass(name, table, kind):
            with ExitStack() as c:
                def sb(nm, shape, dt=F32):
                    return c.enter_context(nc.sbuf_tensor(f"{name}_{nm}", shape, dt))

                def sem(nm):
                    return signal(f"{name}_{nm}")

                msg = sb("msg", [P, EB, D])
                idx = sb("idx", [P, EB], I32)
                fix = sb("fix", [P, D])
                carry = c.enter_context(nc.psum_tensor(f"{name}_carry", [P, 512], F32))
                s_idx = [sem(f"s_idx{k}") for k in range(len(SUBS))]
                s_row = [sem(f"s_row{k}") for k in range(len(SUBS))]
                s_out = [sem(f"s_out{k}") for k in range(len(SUBS))]
                s_mul = sem("s_mul")
                s_sum = sem("s_sum")
                s_go = sem("s_go")
                s_car = sem("s_car")
                s_fg = sem("s_fg")
                s_fa = sem("s_fa")
                s_fs = sem("s_fs")
                block = c.enter_context(nc.Block())
                weighted = kind != "plain"

                @block.gpsimd
                def _(pool):
                    def gather(i, k, first):
                        lo, hi = SUBS[k]
                        if not first:
                            pool.wait_ge(s_out[k], i * 16)
                            if k < len(SUBS) - 1:
                                pool.wait_ge(s_sum, (i - 1) * EB + (hi + 1))
                            else:
                                pool.wait_ge(s_sum, i * EB + 1)
                        pool.wait_ge(s_idx[k], i + 1)
                        nc.gpsimd.nop(nofuse=True)
                        for b in range(lo, hi):
                            nc.gpsimd.indirect_dma_start(
                                msg[:, b, :], None, table,
                                bass.IndirectOffsetOnAxis(ap=idx[:, b:b + 1], axis=0)).then_inc(s_row[k], 16)

                    pool.wait_ge(s_go, 1)
                    for k in range(len(SUBS)):
                        gather(0, k, True)
                    with pool.Fori(1, ESTEPS) as i:
                        for k in range(len(SUBS)):
                            gather(i, k, False)
                    for k in range(len(SUBS)):
                        pool.wait_ge(s_out[k], ESTEPS * 16)
                    nc.gpsimd.indirect_dma_start(
                        fix[:, :], None, tot, bass.IndirectOffsetOnAxis(ap=fix_i[:, 0:1], axis=0)).then_inc(s_fg, 16)
                    pool.wait_ge(s_fa, 1)
                    nc.gpsimd.indirect_dma_start(
                        tot, bass.IndirectOffsetOnAxis(ap=fix_i[:, 0:1], axis=0), fix[:, :], None).then_inc(s_fs, 16)
                    pool.wait_ge(s_fs, 16)

                @block.sync
                def _(sp):
                    rows = tot[0:P * EC, :].rearrange("(p t) d -> p t d", t=EC)

                    def store(i, k):
                        lo, hi = SUBS[k]
                        sp.wait_ge(s_sum, i * EB + hi)
                        sp.dma_start(rows[:, bass.ds(i * EB + lo, hi - lo), :], msg[:, lo:hi, :]).then_inc(s_out[k], 16)

                    with sp.Fori(0, ESTEPS) as i:
                        for k in range(len(SUBS)):
                            store(i, k)
                    for k in range(len(SUBS)):
                        sp.wait_ge(s_out[k], ESTEPS * 16)

                @block.vector
                def _(dve):
                    v = nc.vector

                    def stage(i, k):
                        lo, hi = SUBS[k]
                        v.tensor_copy(idx[:, lo:hi], src_i[:, bass.ds(i * EB + lo, hi - lo)]).then_inc(s_idx[k], 1)

                    def column(i, b, first):
                        if kind == "weight":
                            v.tensor_scalar(msg[:, b, :], msg[:, b, :], wgt[:, bass.ds(i * EB + b, 1)], None,
                                            ALU.mult).then_inc(s_mul, 1)
                        elif kind == "alpha":
                            m = msg[:, b, :].rearrange("p (h o) -> p h o", h=H)
                            a = alpha[:, :, bass.ds(i * EB + b, 1)]
                            v.tensor_tensor(m, m, a.broadcast_to([P, H, HD]), ALU.mult).then_inc(s_mul, 1)
                        if weighted:
                            dve.wait_ge(s_mul, i * EB + (b + 1))
                        if not (first and b == 0):
                            dve.wait_ge(s_sum, i * EB + b)
                        v.scalar_tensor_tensor(
                            msg[:, b, :], msg[:, (b - 1) % EB, :] if not (first and b == 0) else msg[:, b, :],
                            same[:, bass.ds(i * EB + b, 1)], msg[:, b, :], ALU.mult, ALU.add).then_inc(s_sum, 1)

                    def step(i, first):
                        for k, (lo, hi) in enumerate(SUBS):
                            dve.wait_ge(s_row[k], (i + 1) * (16 * (hi - lo)))
                            stage(i + 1, k)
                            for b in range(lo, hi):
                                column(i, b, first)

                    v.memset(fix[:, :], 0.0).then_inc(s_go, 1)
                    for k in range(len(SUBS)):
                        stage(0, k)
                    step(0, True)
                    with dve.Fori(1, ESTEPS) as i:
                        step(i, False)
                    dve.wait_ge(s_car, 1)
                    dve.wait_ge(s_fg, 16)
                    v.tensor_tensor(fix[:, :], fix[:, :], carry[:, 0:D], ALU.add).then_inc(s_fa, 1)

                @block.tensor
                def _(pe):
                    pe.wait_ge(s_sum, EC)
                    nc.tensor.matmul(carry[:, 0:D], carryT[:, :], msg[:, EB - 1, :], start=True,
                                     stop=True).then_inc(s_car, 1)

        def nodes(table, st):
            if st.tiles == 1:
                return table[GROUPS * GN:GROUPS * GN + TAILN, :].rearrange("(j p) d -> p j d", j=1)
            return table[bass.ds(st.g * GN, GN), :].rearrange("(j p) d -> p j d", p=P)

        def group_T(st, buf):
            if st.tiles == 1:
                return (hT[GROUPS, :, 0:KC * TAILN].rearrange("p (c n) -> p c n", c=KC), buf[:, :, 0:TAILN])
            return hT[bass.ds(st.g, 1), :, :].rearrange("a p (c n) -> (a p) c n", c=KC), buf[:, :, :]

        class Pass:

            def __init__(self, c, name):
                self.c, self.name = c, name

            def sb(self, nm, shape, dt=F32):
                return self.c.enter_context(nc.sbuf_tensor(f"{self.name}_{nm}", shape, dt))

            def ps(self, nm, shape):
                return self.c.enter_context(nc.psum_tensor(f"{self.name}_{nm}", shape, F32))

            def sem(self, nm):
                return signal(f"{self.name}_{nm}")

            def sb2(self, nm, shape, dt=F32):
                return [self.sb(f"{nm}{i}", shape, dt) for i in range(2)]

            def ps2(self, nm, shape):
                return [self.ps(f"{nm}{i}", shape) for i in range(2)]

            def sem2(self, nm):
                return [self.sem(f"{nm}{i}") for i in range(2)]

        def gather_last(pool, st, agg, nidx, s_ni, s_agg, s_used):
            if not st.first:
                pool.wait_ge(s_agg[st.par], st.use * (16 * G))
                nc.gpsimd.nop(nofuse=True)
            nc.gpsimd.tensor_copy(nidx[st.par][:, 0:st.tiles],
                                  nlast[:, bass.ds(st.g * G, st.tiles)]).then_inc(s_ni[st.par], 1)
            if not st.first:
                pool.wait_ge(s_used[st.par], done(st.use - 1))
            pool.wait_ge(s_ni[st.par], done(st.use))
            nc.gpsimd.nop(nofuse=True)
            for j in range(st.tiles):
                nc.gpsimd.indirect_dma_start(
                    agg[st.par][0:st.rows, j, :], None, tot,
                    bass.IndirectOffsetOnAxis(ap=nidx[st.par][0:st.rows, j:j + 1], axis=0)).then_inc(s_agg[st.par], 16)

        def agg_done(st):
            return (st.use * G + st.tiles) * 16

        def batch_norm_params(dve_chain, v, which, stats, mv, gam, bet, tmp, act_sqrt, cols):
            link, wait_sqrt = dve_chain
            for cc in range(KC):
                link(v.bn_aggr(mv[:, cc, :], stats[:, cc, 0:cols, :].rearrange("p a b -> p (a b)")))
            link(v.tensor_scalar(tmp[:, 0:KC], mv[:, :, 1], EPS, None, ALU.add))
            act_sqrt()
            wait_sqrt()
            link(v.reciprocal(tmp[:, 0:KC], tmp[:, 0:KC]))
            link(v.tensor_tensor(bn[:, which, 0, :], tmp[:, 0:KC], gam[:, :], ALU.mult))
            link(v.tensor_tensor(tmp[:, 0:KC], mv[:, :, 0], bn[:, which, 0, :], ALU.mult))
            link(v.tensor_tensor(bn[:, which, 1, :], bet[:, :], tmp[:, 0:KC], ALU.subtract))

        def column(flat):
            return flat.rearrange("(c p) -> p c", p=P)

        def mlp_in(name, rows_in, norm_layer, w1T, gamma, beta, which, bias=None, store_rows=None):
            with ExitStack() as c:
                p = Pass(c, name)
                x = p.sb2("x", [P, G, D])
                agg = p.sb2("agg", [P, G, D])
                y = p.sb2("y", [P, G, D])
                yT = p.sb2("yT", [P, KC, GN])
                h = p.sb2("h", [P, KC, GN])
                nidx = p.sb2("nidx", [P, G], I32)
                w = p.sb("w", [P, KC, D])
                gam, bet, bia = p.sb("gam", [P, KC]), p.sb("bet", [P, KC]), p.sb("bia", [P, KC])
                epsw = p.sb("epsw", [P, 1])
                stats = p.sb("stats", [P, KC, GROUPS + 1, 6])
                mv = p.sb("mv", [P, KC, 2])
                tmp = p.sb("tmp", [P, KC])
                ln = p.sb2("ln", [P, G, 6])
                lmv = p.sb2("lmv", [P, G, 2])
                rstd = p.sb2("rstd", [P, G])
                vv = p.sb2("vv", [P, G, D]) if norm_layer else None
                nmr = p.sb2("nmr", [P, G])
                yb = p.sb2("yb", [P, G, D]) if norm_layer else None
                bg = p.sb("bg", [P, D]) if norm_layer else None
                yps = p.ps2("yps", [P, KC, 512])
                hps = p.ps2("hps", [P, KC, 512])
                s_w = p.sem("s_w")
                s_x = p.sem2("s_x")
                s_ni = p.sem2("s_ni")
                s_agg = p.sem2("s_agg")
                s_go = p.sem("s_go")
                s_in = p.sem2("s_in")
                s_lv = p.sem2("s_lv")
                s_var = p.sem2("s_var")
                s_sd = p.sem2("s_sd")
                s_y = p.sem2("s_y")
                s_fac = p.sem2("s_fac")
                s_yb = p.sem2("s_yb")
                s_tr = p.sem2("s_tr")
                s_yT = p.sem2("s_yT")
                s_mm = p.sem2("s_mm")
                s_h = p.sem2("s_h")
                s_st = p.sem2("s_st")
                s_ho = p.sem2("s_ho")
                s_yo = p.sem2("s_yo")
                s_ch = p.sem("s_ch")
                s_q = p.sem("s_q")
                s_qd = p.sem("s_qd")
                block = c.enter_context(nc.Block())
                nw = 4 + (1 if bias is not None else 0) + (1 if norm_layer else 0)
                lag = 1 if norm_layer else 0

                @block.sync
                def _(sp):
                    sp.dma_start(w[:, :, :], w1T.rearrange("(c p) n -> p c n", p=P)).then_inc(s_w, 16)
                    with nc.allow_non_contiguous_dma(reason="small vectors"):
                        sp.dma_start(gam[:, :], column(gamma)).then_inc(s_w, 16)
                        sp.dma_start(bet[:, :], column(beta)).then_inc(s_w, 16)
                        if bias is not None:
                            sp.dma_start(bia[:, :], column(bias)).then_inc(s_w, 16)
                    if norm_layer:
                        sp.dma_start(bg[:, :], io["L2_gnn_b_gcn"].rearrange("(a d) -> a d", a=1)
                                     .broadcast_to([P, D])).then_inc(s_w, 16)
                    sp.dma_start(epsw[:, :], io["L0_gnn_eps_weight"].rearrange("(a d) -> a d", a=1)
                                 .broadcast_to([P, 1])).then_inc(s_w, 16)

                    def load(st):
                        if not st.first:
                            sp.wait_ge(s_in[st.par], done(st.use - 1))
                        sp.dma_start(x[st.par][0:st.rows, 0:st.tiles, :], nodes(rows_in, st)).then_inc(s_x[st.par], 16)

                    node_pass(sp, (0, load))

                @block.gpsimd
                def _(pool):
                    pool.wait_ge(s_go, 1)
                    node_pass(pool, (0, lambda st: gather_last(pool, st, agg, nidx, s_ni, s_agg, s_in)))

                @block.vector
                def _(dve):
                    v = nc.vector
                    v.memset(tmp[:, :], 0.0).then_inc(s_go, 1)
                    dve.wait_ge(s_w, 16 * nw)

                    def combine(st):
                        q = st.par
                        xs, ags = x[q][0:st.rows, 0:st.tiles, :], agg[q][0:st.rows, 0:st.tiles, :]
                        dve.wait_ge(s_x[q], done(st.use, 16))
                        dve.wait_ge(s_agg[q], agg_done(st))
                        if not norm_layer:
                            if not st.first:
                                dve.wait_ge(s_tr[q], done(st.use - 1))
                            v.scalar_tensor_tensor(y[q][0:st.rows, 0:st.tiles, :], xs, epsw[0:st.rows, 0:1], ags,
                                                   ALU.mult, ALU.add).then_inc(s_in[q], 1)
                            return
                        if not st.first:
                            dve.wait_ge(s_y[q], done(st.use - 1))
                        v.tensor_tensor(vv[q][0:st.rows, 0:st.tiles, :], xs, ags, ALU.add).then_inc(s_in[q], 1)
                        dve.wait_ge(s_in[q], done(st.use))
                        for j in range(st.tiles):
                            ins = v.bn_stats(ln[q][0:st.rows, j, :], vv[q][0:st.rows, j, :])
                        ins.then_inc(s_lv[q], 1)
                        dve.wait_ge(s_lv[q], st.use * 2 + 1)
                        v.nop(nofuse=True)
                        for j in range(st.tiles):
                            ins = v.bn_aggr(lmv[q][0:st.rows, j, :], ln[q][0:st.rows, j, :])
                        ins.then_inc(s_var[q], 1)

                    def factors(st):
                        q = st.par
                        dve.wait_ge(s_sd[q], done(st.use))
                        v.reciprocal(rstd[q][0:st.rows, 0:st.tiles], rstd[q][0:st.rows, 0:st.tiles]).then_inc(s_lv[q], 1)
                        dve.wait_ge(s_lv[q], st.use * 2 + 2)
                        v.scalar_tensor_tensor(nmr[q][0:st.rows, 0:st.tiles], lmv[q][0:st.rows, 0:st.tiles, 0], -1.0,
                                               rstd[q][0:st.rows, 0:st.tiles], ALU.mult, ALU.mult).then_inc(s_fac[q], 1)

                    def residual(st):
                        q = st.par
                        dve.wait_ge(s_y[q], done(st.use))
                        if not st.first:
                            dve.wait_ge(s_yo[q], done(st.use - 1, 16))
                        b = bg[0:st.rows, :].rearrange("p (a d) -> p a d", a=1).broadcast_to([st.rows, st.tiles, D])
                        v.tensor_tensor(yb[q][0:st.rows, 0:st.tiles, :], y[q][0:st.rows, 0:st.tiles, :], b,
                                        ALU.add).then_inc(s_yb[q], 1)

                    def statistics(st):
                        q = st.par
                        dve.wait_ge(s_h[q], done(st.use))
                        for cc in range(KC):
                            ins = v.bn_stats(stats[:, cc, bass.ds(st.g, 1), :].rearrange("p a b -> p (a b)"),
                                             h[q][:, cc, 0:st.n])
                        ins.then_inc(s_st[q], 1)

                    node_pass(dve, *(([(2, residual)] if norm_layer else []) + [(lag + 3, statistics)]
                                     + ([(1, factors)] if norm_layer else []) + [(0, combine)]))
                    dve.wait_ge(s_st[0], PAIRS + 1)
                    dve.wait_ge(s_st[1], PAIRS)
                    n = [0]

                    def link(ins):
                        n[0] += 1
                        ins.then_inc(s_ch, 1)
                        dve.wait_ge(s_ch, n[0])

                    batch_norm_params((link, lambda: dve.wait_ge(s_qd, 1)), v, which, stats, mv, gam, bet, tmp,
                                      lambda: v.memset(mv[:, 0, 1:2], 0.0).then_inc(s_q, 1), GROUPS + 1)

                @block.tensor
                def _(pe):
                    pe.wait_ge(s_w, 16 * nw)

                    def transpose(st):
                        q = st.par
                        pe.wait_ge((s_y if norm_layer else s_in)[q], done(st.use))
                        if not st.first:
                            pe.wait_ge(s_yT[q], done(st.use - 1))
                        for j in range(st.tiles):
                            for k in range(KC):
                                ins = nc.tensor.transpose(yps[q][:, k, j * P:j * P + st.rows],
                                                          y[q][0:st.rows, j, k * P:(k + 1) * P],
                                                          ident[0:st.rows, 0:st.rows])
                        ins.then_inc(s_tr[q], 1)

                    def product(st):
                        q = st.par
                        pe.wait_ge(s_yT[q], done(st.use))
                        if not st.first:
                            pe.wait_ge(s_h[q], done(st.use - 1))
                        for cc in range(KC):
                            for k in range(KC):
                                ins = nc.tensor.matmul(hps[q][:, cc, 0:st.n], w[:, k, cc * P:(cc + 1) * P],
                                                       yT[q][:, k, 0:st.n], start=(k == 0), stop=(k == KC - 1))
                        ins.then_inc(s_mm[q], 1)

                    node_pass(pe, (lag + 2, product), (lag, transpose))

                @block.scalar
                def _(act):
                    act.wait_ge(s_w, 16 * nw)

                    def deviation(st):
                        q = st.par
                        act.wait_ge(s_var[q], done(st.use))
                        nc.scalar.activation(rstd[q][0:st.rows, 0:st.tiles], lmv[q][0:st.rows, 0:st.tiles, 1], ACT.Sqrt,
                                             bias=eps_t[0:st.rows, 0:1]).then_inc(s_sd[q], 1)

                    def normalise(st):
                        q = st.par
                        act.wait_ge(s_fac[q], done(st.use))
                        if not st.first:
                            act.wait_ge(s_tr[q], done(st.use - 1))
                            act.wait_ge(s_yb[q], done(st.use - 1))
                        for j in range(st.tiles):
                            ins = nc.scalar.activation(y[q][0:st.rows, j, :], vv[q][0:st.rows, j, :], ACT.Identity,
                                                       bias=nmr[q][0:st.rows, j:j + 1], scale=rstd[q][0:st.rows, j:j + 1])
                        ins.then_inc(s_y[q], 1)

                    def copy_T(st):
                        q = st.par
                        act.wait_ge(s_tr[q], done(st.use))
                        if not st.first:
                            act.wait_ge(s_mm[q], done(st.use - 1))
                        nc.scalar.copy(yT[q][:, :, 0:st.n], yps[q][:, :, 0:st.n]).then_inc(s_yT[q], 1)

                    def store(st):
                        q = st.par
                        act.wait_ge(s_yb[q], done(st.use))
                        act.dma_start(nodes(store_rows, st), yb[q][0:st.rows, 0:st.tiles, :]).then_inc(s_yo[q], 16)

                    def copy_h(st):
                        q = st.par
                        act.wait_ge(s_mm[q], done(st.use))
                        if not st.first:
                            act.wait_ge(s_ho[q], done(st.use - 1, 16))
                            act.wait_ge(s_st[q], done(st.use - 1))
                        if bias is None:
                            nc.scalar.copy(h[q][:, :, 0:st.n], hps[q][:, :, 0:st.n]).then_inc(s_h[q], 1)
                        else:
                            nc.scalar.activation(h[q][:, 0, 0:st.n], hps[q][:, 0, 0:st.n], ACT.Identity, bias=bia[:, 0:1])
                            nc.scalar.activation(h[q][:, 1, 0:st.n], hps[q][:, 1, 0:st.n], ACT.Identity,
                                                 bias=bia[:, 1:2]).then_inc(s_h[q], 1)
                        act.wait_ge(s_h[q], done(st.use))
                        dst, part = group_T(st, h[q])
                        act.dma_start(dst, part).then_inc(s_ho[q], 16)

                    if norm_layer:
                        node_pass(act, (1, normalise), (3, copy_h), (2, store), (1, copy_T), (0, deviation))
                    else:
                        node_pass(act, (2, copy_h), (0, copy_T))
                    act.wait_ge(s_q, 1)
                    nc.scalar.activation(tmp[:, 0:KC], tmp[:, 0:KC], ACT.Sqrt).then_inc(s_qd, 1)
                    for q, uses in ((0, PAIRS + 1), (1, PAIRS)):
                        act.wait_ge(s_ho[q], uses * 16)
                        if norm_layer:
                            act.wait_ge(s_yo[q], uses * 16)

        eps_t = keep("eps_t", [P, 1])

        def mlp0_out():
            with ExitStack() as c:
                p = Pass(c, "b")
                hin = p.sb2("hin", [P, KC, GN])
                a = p.sb2("a", [P, KC, GN])
                y2 = p.sb2("y2", [P, KC, GN])
                nrow = p.sb2("nrow", [1, GN])
                nb = p.sb2("nb", [P, GN])
                w = p.sb("w", [P, KC, D])
                gam, bet = p.sb("gam", [P, KC]), p.sb("bet", [P, KC])
                stats = p.sb("stats", [P, KC, GROUPS + 1, 6])
                mv = p.sb("mv", [P, KC, 2])
                tmp = p.sb("tmp", [P, KC])
                ps = p.ps2("ps", [P, KC, 512])
                s_w = p.sem("s_w")
                s_hin, s_nr, s_nb, s_a = p.sem2("s_hin"), p.sem2("s_nr"), p.sem2("s_nb"), p.sem2("s_a")
                s_mm, s_y2, s_st, s_o = p.sem2("s_mm"), p.sem2("s_y2"), p.sem2("s_st"), p.sem2("s_o")
                s_ch, s_q, s_qd = p.sem("s_ch"), p.sem("s_q"), p.sem("s_qd")
                block = c.enter_context(nc.Block())
                nflat = nnd.rearrange("t p -> (t p)")

                @block.sync
                def _(sp):
                    sp.dma_start(w[:, :, :], io["L0_gnn_w2T"].rearrange("(c p) n -> p c n", p=P)).then_inc(s_w, 16)
                    with nc.allow_non_contiguous_dma(reason="small vectors"):
                        sp.dma_start(gam[:, :], column(io["L0_gnn_gamma_h"])).then_inc(s_w, 16)
                        sp.dma_start(bet[:, :], column(io["L0_gnn_beta_h"])).then_inc(s_w, 16)

                    def load(st):
                        q = st.par
                        if not st.first:
                            sp.wait_ge(s_a[q], done(st.use - 1))
                        src, part = group_T(st, hin[q])
                        sp.dma_start(part, src).then_inc(s_hin[q], 16)
                        if not st.first:
                            sp.wait_ge(s_nb[q], done(st.use - 1))
                        n = nflat[bass.ds(st.g * GN, st.n)].rearrange("(a n) -> a n", a=1)
                        sp.dma_start(nrow[q][0:1, 0:st.n], n).then_inc(s_nr[q], 16)

                    def store(st):
                        q = st.par
                        sp.wait_ge(s_y2[q], done(st.use))
                        dst, part = group_T(st, y2[q])
                        sp.dma_start(dst, part).then_inc(s_o[q], 16)

                    node_pass(sp, (0, load), (4, store))
                    sp.wait_ge(s_o[0], 16 * (PAIRS + 1))
                    sp.wait_ge(s_o[1], 16 * PAIRS)

                @block.gpsimd
                def _(pool):
                    def spread(st):
                        q = st.par
                        if not st.first:
                            pool.wait_ge(s_y2[q], done(st.use - 1))
                        pool.wait_ge(s_nr[q], done(st.use, 16))
                        nc.gpsimd.nop(nofuse=True)
                        nc.gpsimd.partition_broadcast(nb[q][:, 0:st.n], nrow[q][0:1, 0:st.n]).then_inc(s_nb[q], 1)

                    node_pass(pool, (0, spread))

                @block.scalar
                def _(act):
                    def relu(st):
                        q = st.par
                        act.wait_ge(s_hin[q], done(st.use, 16))
                        if not st.first:
                            act.wait_ge(s_mm[q], done(st.use - 1))
                        for cc in range(KC):
                            ins = nc.scalar.activation(a[q][:, cc, 0:st.n], hin[q][:, cc, 0:st.n], ACT.Relu,
                                                       bias=bn[:, 0, 1, cc:cc + 1], scale=bn[:, 0, 0, cc:cc + 1])
                        ins.then_inc(s_a[q], 1)

                    node_pass(act, (0, relu))
                    act.wait_ge(s_q, 1)
                    nc.scalar.activation(tmp[:, 0:KC], tmp[:, 0:KC], ACT.Sqrt).then_inc(s_qd, 1)

                @block.tensor
                def _(pe):
                    pe.wait_ge(s_w, 48)

                    def product(st):
                        q = st.par
                        pe.wait_ge(s_a[q], done(st.use))
                        if not st.first:
                            pe.wait_ge(s_y2[q], done(st.use - 1))
                        for cc in range(KC):
                            for k in range(KC):
                                ins = nc.tensor.matmul(ps[q][:, cc, 0:st.n], w[:, k, cc * P:(cc + 1) * P],
                                                       a[q][:, k, 0:st.n], start=(k == 0), stop=(k == KC - 1))
                        ins.then_inc(s_mm[q], 1)

                    node_pass(pe, (0, product))

                @block.vector
                def _(dve):
                    v = nc.vector

                    def scale(st):
                        q = st.par
                        dve.wait_ge(s_mm[q], done(st.use))
                        dve.wait_ge(s_nb[q], done(st.use))
                        if not st.first:
                            dve.wait_ge(s_o[q], done(st.use - 1, 16))
                            dve.wait_ge(s_st[q], done(st.use - 1))
                        b = nb[q][:, 0:st.n].rearrange("p (a n) -> p a n", a=1).broadcast_to([P, KC, st.n])
                        v.tensor_tensor(y2[q][:, :, 0:st.n], ps[q][:, :, 0:st.n], b, ALU.mult).then_inc(s_y2[q], 1)

                    def statistics(st):
                        q = st.par
                        dve.wait_ge(s_y2[q], done(st.use))
                        for cc in range(KC):
                            ins = v.bn_stats(stats[:, cc, bass.ds(st.g, 1), :].rearrange("p a b -> p (a b)"),
                                             y2[q][:, cc, 0:st.n])
                        ins.then_inc(s_st[q], 1)

                    node_pass(dve, (1, statistics), (0, scale))
                    dve.wait_ge(s_w, 48)
                    dve.wait_ge(s_st[0], PAIRS + 1)
                    dve.wait_ge(s_st[1], PAIRS)
                    n = [0]

                    def link(ins):
                        n[0] += 1
                        ins.then_inc(s_ch, 1)
                        dve.wait_ge(s_ch, n[0])

                    batch_norm_params((link, lambda: dve.wait_ge(s_qd, 1)), v, 1, stats, mv, gam, bet, tmp,
                                      lambda: v.memset(mv[:, 0, 1:2], 0.0).then_inc(s_q, 1), GROUPS + 1)

        def project():
            with ExitStack() as c:
                p = Pass(c, "c")
                hin = p.sb2("hin", [P, KC, GN])
                r = p.sb2("r", [P, KC, GN])
                x = p.sb2("x", [P, G, D])
                vv = p.sb2("vv", [P, G, D])
                x1 = p.sb2("x1", [P, G, D])
                x1T = p.sb2("x1T", [P, KC, GN])
                z = p.sb2("z", [P, G, D + 2 * H])
                w = p.sb("w", [P, KC, D + 2 * H])
                av = p.sb("av", [P, 2, D])
                wa = p.sb("wa", [P, D])
                ln, lmv, rstd = p.sb2("ln", [P, G, 6]), p.sb2("lmv", [P, G, 2]), p.sb2("rstd", [P, G])
                rps = p.ps("rps", [P, 2, 512])
                xps = p.ps("xps", [P, KC, 512])
                zps = [p.ps(f"zps{j}", [P, 512]) for j in range(G)]
                s_w, s_wa = p.sem("s_w"), p.sem("s_wa")
                s_hin, s_x, s_r, s_rt = p.sem2("s_hin"), p.sem2("s_x"), p.sem2("s_r"), p.sem2("s_rt")
                s_lv, s_var, s_sd, s_vu, s_x1 = (p.sem2("s_lv"), p.sem2("s_var"), p.sem2("s_sd"), p.sem2("s_vu"),
                                                 p.sem2("s_x1"))
                s_xo, s_tr, s_xT = p.sem2("s_xo"), p.sem2("s_tr"), p.sem2("s_xT")
                s_mm = p.sem2("s_mm")
                s_z = p.sem2("s_z")
                s_zo, s_sc = p.sem2("s_zo"), p.sem2("s_sc")
                s_m, s_wm, s_end = p.sem("s_m"), p.sem("s_wm"), p.sem("s_end")
                block = c.enter_context(nc.Block())

                @block.sync
                def _(sp):
                    sp.dma_start(w[:, :, 0:D], io["L1_gnn_W_flat"].rearrange("(c p) n -> p c n", p=P)).then_inc(s_w, 16)
                    for k, nm in enumerate(("L1_gnn_a_src", "L1_gnn_a_dst")):
                        sp.dma_start(av[:, k, :], io[nm].rearrange("(a h) o -> a (h o)", a=1).broadcast_to([P, D])
                                     ).then_inc(s_w, 16)

                    def load(st):
                        q = st.par
                        if not st.first:
                            sp.wait_ge(s_r[q], done(st.use - 1))
                        src, part = group_T(st, hin[q])
                        sp.dma_start(part, src).then_inc(s_hin[q], 16)
                        if not st.first:
                            sp.wait_ge(s_vu[q], done(st.use - 1))
                        sp.dma_start(x[q][0:st.rows, 0:st.tiles, :], nodes(io["x"], st)).then_inc(s_x[q], 16)

                    node_pass(sp, (0, load))
                    sp.wait_ge(s_sc[0], PAIRS + 1)
                    sp.wait_ge(s_sc[1], PAIRS)
                    sp.dma_start(esd.rearrange("(p t) e -> p (t e)", t=NT),
                                 scores[:, :, :].rearrange("p t e -> p (t e)")).then_inc(s_end, 16)
                    sp.wait_ge(s_end, 16)

                @block.gpsimd
                def _(pool):
                    nc.gpsimd.memset(scores[:, NT - 1, :], 0.0).then_inc(s_m, 1)
                    pool.wait_ge(s_m, 1)

                    def keep_scores(st):
                        q = st.par
                        pool.wait_ge(s_z[q], st.use * G + st.tiles)
                        nc.gpsimd.nop(nofuse=True)
                        nc.gpsimd.tensor_copy(scores[0:st.rows, bass.ds(st.g * G, st.tiles), :],
                                              z[q][0:st.rows, 0:st.tiles, D:D + 2 * H]).then_inc(s_sc[q], 1)

                    node_pass(pool, (4, keep_scores))

                @block.scalar
                def _(act):
                    def relu(st):
                        q = st.par
                        act.wait_ge(s_hin[q], done(st.use, 16))
                        if not st.first:
                            act.wait_ge(s_rt[q], done(st.use - 1))
                        for cc in range(KC):
                            ins = nc.scalar.activation(r[q][:, cc, 0:st.n], hin[q][:, cc, 0:st.n], ACT.Relu,
                                                       bias=bn[:, 1, 1, cc:cc + 1], scale=bn[:, 1, 0, cc:cc + 1])
                        ins.then_inc(s_r[q], 1)

                    def deviation(st):
                        q = st.par
                        act.wait_ge(s_var[q], done(st.use))
                        nc.scalar.activation(rstd[q][0:st.rows, 0:st.tiles], lmv[q][0:st.rows, 0:st.tiles, 1], ACT.Sqrt,
                                             bias=eps_t[0:st.rows, 0:1]).then_inc(s_sd[q], 1)

                    def copy_T(st):
                        q = st.par
                        act.wait_ge(s_x1[q], done(st.use))
                        act.dma_start(nodes(x1d, st), x1[q][0:st.rows, 0:st.tiles, :]).then_inc(s_xo[q], 16)
                        act.wait_ge(s_tr[q], done(st.use))
                        if not st.first:
                            act.wait_ge(s_mm[q], st.use * G)
                        nc.scalar.copy(x1T[q][:, :, 0:st.n], xps[:, :, 0:st.n]).then_inc(s_xT[q], 1)

                    def copy_z(st):
                        q = st.par
                        if not st.first:
                            act.wait_ge(s_zo[q], done(st.use - 1, 16))
                            act.wait_ge(s_sc[q], done(st.use - 1))
                        for j in range(st.tiles):
                            act.wait_ge(s_mm[q], st.use * G + (j + 1))
                            nc.scalar.copy(z[q][0:st.rows, j, :], zps[j][0:st.rows, 0:D + 2 * H]).then_inc(s_z[q], 1)
                        act.wait_ge(s_z[q], st.use * G + st.tiles)
                        act.dma_start(nodes(zd, st), z[q][0:st.rows, 0:st.tiles, 0:D]).then_inc(s_zo[q], 16)

                    node_pass(act, (0, relu), (4, copy_z), (2, copy_T), (1, deviation))
                    for q, uses in ((0, PAIRS + 1), (1, PAIRS)):
                        act.wait_ge(s_xo[q], uses * 16)
                        act.wait_ge(s_zo[q], uses * 16)

                @block.tensor
                def _(pe):
                    pe.wait_ge(s_wa, 5)

                    def back(st):
                        q = st.par
                        pe.wait_ge(s_r[q], done(st.use))
                        if not st.first or st.par == 1:
                            if st.par == 0:
                                pe.wait_ge(s_vu[1], done(st.use - 1))
                            else:
                                pe.wait_ge(s_vu[0], done(st.use))
                        for j in range(st.tiles):
                            for k in range(KC):
                                col = j * D + k * P
                                ins = nc.tensor.transpose(rps[0:st.rows, col // 512, col % 512:col % 512 + P],
                                                          r[q][:, k, j * P:j * P + st.rows], ident[:, :])
                        ins.then_inc(s_rt[q], 1)

                    def transpose(st):
                        q = st.par
                        pe.wait_ge(s_x1[q], done(st.use))
                        if not st.first or st.par == 1:
                            if st.par == 0:
                                pe.wait_ge(s_xT[1], done(st.use - 1))
                            else:
                                pe.wait_ge(s_xT[0], done(st.use))
                        for j in range(st.tiles):
                            for k in range(KC):
                                ins = nc.tensor.transpose(xps[:, k, j * P:j * P + st.rows],
                                                          x1[q][0:st.rows, j, k * P:(k + 1) * P],
                                                          ident[0:st.rows, 0:st.rows])
                        ins.then_inc(s_tr[q], 1)

                    def product(st):
                        q = st.par
                        pe.wait_ge(s_xT[q], done(st.use))
                        for j in range(st.tiles):
                            if not st.first or st.par == 1:
                                if st.par == 0:
                                    pe.wait_ge(s_z[1], (st.use - 1) * G + (j + 1))
                                else:
                                    pe.wait_ge(s_z[0], st.use * G + (j + 1))
                            for k in range(KC):
                                ins = nc.tensor.matmul(zps[j][0:st.rows, 0:D + 2 * H],
                                                       x1T[q][:, k, j * P:j * P + st.rows], w[:, k, :],
                                                       start=(k == 0), stop=(k == KC - 1))
                            ins.then_inc(s_mm[q], 1)

                    node_pass(pe, (4, product), (2, transpose), (0, back))

                @block.vector
                def _(dve):
                    v = nc.vector
                    dve.wait_ge(s_w, 48)
                    n = 0
                    for k in range(KC):
                        for e in range(2):
                            if n:
                                dve.wait_ge(s_wa, n)
                            v.tensor_tensor(wa[:, :], w[:, k, 0:D], av[:, e, :], ALU.mult).then_inc(s_wm, 1)
                            dve.wait_ge(s_wm, n + 1)
                            v.tensor_reduce(w[:, k, D + e * H:D + (e + 1) * H],
                                            wa[:, :].rearrange("p (h o) -> p h o", h=H), AX.X, ALU.add).then_inc(s_wa, 1)
                            n += 1
                    dve.wait_ge(s_wa, 4)
                    v.memset(wa[:, :], 0.0).then_inc(s_wa, 1)

                    def combine(st):
                        q = st.par
                        dve.wait_ge(s_x[q], done(st.use, 16))
                        dve.wait_ge(s_rt[q], done(st.use))
                        rows = rps[0:st.rows, :, :].rearrange("p a b -> p (a b)")[:, 0:st.tiles * D]
                        v.scalar_tensor_tensor(vv[q][0:st.rows, 0:st.tiles, :].rearrange("p a b -> p (a b)"),
                                               x[q][0:st.rows, 0:st.tiles, :].rearrange("p a b -> p (a b)"),
                                               2.0, rows, ALU.mult, ALU.add).then_inc(s_vu[q], 1)
                        dve.wait_ge(s_vu[q], done(st.use))
                        for j in range(st.tiles):
                            ins = v.bn_stats(ln[q][0:st.rows, j, :], vv[q][0:st.rows, j, :])
                        ins.then_inc(s_lv[q], 1)
                        dve.wait_ge(s_lv[q], st.use * 2 + 1)
                        v.nop(nofuse=True)
                        for j in range(st.tiles):
                            ins = v.bn_aggr(lmv[q][0:st.rows, j, :], ln[q][0:st.rows, j, :])
                        ins.then_inc(s_var[q], 1)

                    def normalise(st):
                        q = st.par
                        dve.wait_ge(s_sd[q], done(st.use))
                        v.reciprocal(rstd[q][0:st.rows, 0:st.tiles], rstd[q][0:st.rows, 0:st.tiles]).then_inc(s_lv[q], 1)
                        dve.wait_ge(s_lv[q], st.use * 2 + 2)
                        if not st.first:
                            dve.wait_ge(s_tr[q], done(st.use - 1))
                            dve.wait_ge(s_xo[q], done(st.use - 1, 16))
                        for j in range(st.tiles):
                            ins = v.tensor_scalar(x1[q][0:st.rows, j, :], vv[q][0:st.rows, j, :],
                                                  lmv[q][0:st.rows, j, 0:1], rstd[q][0:st.rows, j:j + 1],
                                                  ALU.subtract, ALU.mult)
                        ins.then_inc(s_x1[q], 1)

                    node_pass(dve, (2, normalise), (1, combine))

        def attention():
            with ExitStack() as c:
                p = Pass(c, "att")
                rs = p.sb("rs", [P, EB, 2 * H])
                rd = p.sb("rd", [P, EB, 2 * H])
                ids = p.sb("ids", [P, EB], I32)
                idd = p.sb("idd", [P, EB], I32)
                e = p.sb("e", [P, H, EC])
                f = p.sb("f", [P, H, EC])
                r = p.sb("r", [P, H, EC])
                nxt = p.sb("nxt", [P, EC])
                endr = p.sb("endr", [P, EC])
                pen = p.sb("pen", [P, EC])
                pen4 = p.sb("pen4", [P, 4, P])
                diag = p.sb("diag", [P, 2, H, P])
                com = p.sb("com", [P, H, P])
                part = p.sb("part", [P, 4, H])
                ends = p.sb("ends", [P, 2, H])
                rows = p.ps("rows", [P, 2, 512])
                nsub = len(SUBS)
                s_is = [p.sem(f"s_is{k}") for k in range(nsub)]
                s_g = [p.sem(f"s_g{k}") for k in range(nsub)]
                s_e = p.sem("s_e")
                s_c, s_d, s_r, s_x, s_xd = p.sem("s_c"), p.sem("s_d"), p.sem("s_r"), p.sem("s_x"), p.sem("s_xd")
                block = c.enter_context(nc.Block())

                @block.gpsimd
                def _(pool):
                    with pool.Fori(0, ESTEPS) as i:
                        for k, (lo, hi) in enumerate(SUBS):
                            pool.wait_ge(s_is[k], i + 1)
                            nc.gpsimd.nop(nofuse=True)
                            for b in range(lo, hi):
                                for got, idx in ((rs, ids), (rd, idd)):
                                    nc.gpsimd.indirect_dma_start(
                                        got[:, b, :], None, esd,
                                        bass.IndirectOffsetOnAxis(ap=idx[:, b:b + 1], axis=0)).then_inc(s_g[k], 16)

                @block.tensor
                def _(pe):
                    for u in range(2):
                        pe.wait_ge(s_d, u + 1)
                        for k in range(2):
                            ins = nc.tensor.matmul(rows[:, k, :], ones[:, :],
                                                   diag[:, k, :, :].rearrange("p h q -> p (h q)"), start=True, stop=True)
                        ins.then_inc(s_r, 1)

                @block.scalar
                def _(act):
                    act.wait_ge(s_x, 1)
                    nc.scalar.activation(e[:, :, :], e[:, :, :], ACT.Exp).then_inc(s_xd, 1)

                @block.vector
                def _(dve):
                    v = nc.vector

                    def stage(i, k):
                        lo, hi = SUBS[k]
                        v.tensor_copy(ids[:, lo:hi], ssc_i[:, bass.ds(i * EB + lo, hi - lo)])
                        v.tensor_copy(idd[:, lo:hi], dsc_i[:, bass.ds(i * EB + lo, hi - lo)]).then_inc(s_is[k], 1)

                    for k in range(nsub):
                        stage(0, k)
                    with dve.Fori(0, ESTEPS) as i:
                        for k, (lo, hi) in enumerate(SUBS):
                            dve.wait_ge(s_g[k], (i + 1) * (32 * (hi - lo)))
                            v.tensor_tensor(e[:, :, bass.ds(i * EB + lo, hi - lo)], rs[:, lo:hi, 0:H].rearrange("p b h -> p h b"),
                                            rd[:, lo:hi, H:2 * H].rearrange("p b h -> p h b"),
                                            ALU.add).then_inc(s_e, 1)
                            dve.wait_ge(s_e, i * nsub + (k + 1))
                            stage(i + 1, k)
                    n = [0]

                    def link(ins):
                        n[0] += 1
                        ins.then_inc(s_c, 1)
                        dve.wait_ge(s_c, n[0])

                    def flat(t):
                        return t[:, :, :].rearrange("p h t -> p (h t)")

                    link(v.scalar_tensor_tensor(flat(e), flat(e), 0.01, flat(e), ALU.mult, ALU.max))
                    link(v.memset(nxt[:, :], 0.0))
                    link(v.tensor_copy(nxt[:, 0:EC - 1], same[:, 1:EC]))
                    link(v.tensor_scalar(endr[:, :], nxt[:, :], -1.0, 1.0, ALU.mult, ALU.add))
                    link(v.tensor_scalar(pen[:, :], same[:, :], -1.0, BIG, ALU.add, ALU.mult))
                    link(v.tensor_scalar(pen4[:, :, :].rearrange("p a q -> p (a q)"),
                                         fl4[:, :, :].rearrange("p a q -> p (a q)"), -1.0, BIG, ALU.add, ALU.mult))

                    def segment_total(x, op, turn):
                        for h in range(H):
                            if op == ALU.max:
                                link(v.tensor_tensor_scan(f[:, h, :], pen[:, :], x[:, h, :], -BIG, ALU.add, ALU.max))
                            else:
                                link(v.tensor_tensor_scan(f[:, h, :], same[:, :], x[:, h, :], 0.0, ALU.mult, ALU.add))
                            link(v.tensor_copy(ends[:, 0, h:h + 1], f[:, h, EC - 1:EC]))
                            link(v.tensor_tensor(f[:, h, :], f[:, h, :], endr[:, :], ALU.mult))
                            link(v.tensor_tensor_scan(r[:, h, ::-1], nxt[:, ::-1], f[:, h, ::-1], 0.0, ALU.mult, ALU.add))
                            link(v.tensor_copy(ends[:, 1, h:h + 1], r[:, h, 0:1]))
                        for k in range(2):
                            for h in range(H):
                                ins = v.tensor_scalar(diag[:, k, h, :], ident[:, :], ends[:, k, h:h + 1], None, ALU.mult)
                        ins.then_inc(s_d, 1)
                        dve.wait_ge(s_r, turn + 1)
                        for m in range(4):
                            row = rows[:, m % 2, :].rearrange("p (h q) -> p h q", h=H)
                            mask = (pen4 if op == ALU.max else fl4)[:, m:m + 1, :].broadcast_to([P, H, P])
                            link(v.tensor_tensor(com[:, :, :], row, mask, ALU.add if op == ALU.max else ALU.mult))
                            link(v.tensor_reduce(part[:, m, :], com[:, :, :], AX.X, op))
                        for m in range(2):
                            link(v.tensor_tensor(part[:, 2 * m, :], part[:, 2 * m, :], part[:, 2 * m + 1, :], op))
                        for h in range(H):
                            link(v.tensor_tensor(r[:, h, :], r[:, h, :], midrun[:, :], ALU.mult))
                            link(v.scalar_tensor_tensor(r[:, h, :], firstrun[:, :], part[:, 0, h:h + 1], r[:, h, :],
                                                        ALU.mult, ALU.add))
                            link(v.scalar_tensor_tensor(r[:, h, :], lastrun[:, :], part[:, 2, h:h + 1], r[:, h, :],
                                                        ALU.mult, ALU.add))

                    segment_total(e, ALU.max, 0)
                    link(v.tensor_tensor(flat(e), flat(e), flat(r), ALU.subtract))
                    v.memset(com[:, 0, 0:1], 0.0).then_inc(s_x, 1)
                    dve.wait_ge(s_xd, 1)
                    segment_total(e, ALU.add, 1)
                    link(v.reciprocal(flat(r), flat(r)))
                    link(v.tensor_tensor(flat(alpha), flat(e), flat(r), ALU.mult))

        def gcn_table():
            with ExitStack() as c:
                p = Pass(c, "g")
                hin, a, xw = p.sb2("hin", [P, KC, GN]), p.sb2("a", [P, KC, GN]), p.sb2("xw", [P, G, D])
                w2, wg, wc = p.sb("w2", [P, KC, D]), p.sb("wg", [P, KC, D]), p.sb("wc", [P, KC, D])
                b2c, b2b, bc = p.sb("b2c", [P, KC]), p.sb("b2b", [P, KC, P]), p.sb("bc", [P, D])
                ps = p.ps2("ps", [P, 2, 512])
                wps, bps = p.ps("wps", [P, KC, D]), p.ps("bps", [P, 512])
                s_w, s_b2, s_wp, s_wc = p.sem("s_w"), p.sem("s_b2"), p.sem("s_wp"), p.sem("s_wc")
                s_hin, s_a, s_mm, s_sum, s_xw, s_o = (p.sem2("s_hin"), p.sem2("s_a"), p.sem2("s_mm"), p.sem2("s_sum"),
                                                      p.sem2("s_xw"), p.sem2("s_o"))
                block = c.enter_context(nc.Block())

                @block.sync
                def _(sp):
                    sp.dma_start(w2[:, :, :], io["L2_gnn_w2"].rearrange("(c p) n -> p c n", p=P)).then_inc(s_w, 16)
                    sp.dma_start(wg[:, :, :], io["L2_gnn_w_gcnT"].rearrange("(c p) n -> p c n", p=P)).then_inc(s_w, 16)
                    with nc.allow_non_contiguous_dma(reason="small vectors"):
                        sp.dma_start(b2c[:, :], column(io["L2_gnn_b2"])).then_inc(s_w, 16)

                    def load(st):
                        q = st.par
                        if not st.first:
                            sp.wait_ge(s_a[q], done(st.use - 1))
                        src, part = group_T(st, hin[q])
                        sp.dma_start(part, src).then_inc(s_hin[q], 16)

                    def store(st):
                        q = st.par
                        sp.wait_ge(s_xw[q], done(st.use))
                        sp.dma_start(nodes(zd, st), xw[q][0:st.rows, 0:st.tiles, :]).then_inc(s_o[q], 16)

                    node_pass(sp, (0, load), (4, store))
                    sp.wait_ge(s_o[0], 16 * (PAIRS + 1))
                    sp.wait_ge(s_o[1], 16 * PAIRS)

                @block.scalar
                def _(act):
                    def relu(st):
                        q = st.par
                        act.wait_ge(s_hin[q], done(st.use, 16))
                        if not st.first:
                            act.wait_ge(s_mm[q], done(st.use - 1))
                        for cc in range(KC):
                            ins = nc.scalar.activation(a[q][:, cc, 0:st.n], hin[q][:, cc, 0:st.n], ACT.Relu,
                                                       bias=bn[:, 2, 1, cc:cc + 1], scale=bn[:, 2, 0, cc:cc + 1])
                        ins.then_inc(s_a[q], 1)

                    node_pass(act, (0, relu))

                @block.tensor
                def _(pe):
                    pe.wait_ge(s_w, 48)
                    pe.wait_ge(s_b2, 1)
                    for i in range(KC):
                        for m in range(KC):
                            nc.tensor.matmul(wps[:, i, :], w2[:, m, i * P:(i + 1) * P], wg[:, m, :], start=(m == 0),
                                             stop=(m == KC - 1))
                    for m in range(KC):
                        ins = nc.tensor.matmul(bps[:, 0:D], b2b[:, m, :], wg[:, m, :], start=(m == 0), stop=(m == KC - 1))
                    ins.then_inc(s_wp, 1)
                    pe.wait_ge(s_wc, 1)

                    def product(st):
                        q = st.par
                        pe.wait_ge(s_a[q], done(st.use))
                        if not st.first:
                            pe.wait_ge(s_sum[q], done(st.use - 1))
                        for j in range(st.tiles):
                            for k in range(KC):
                                ins = nc.tensor.matmul(ps[q][0:st.rows, j // 2, (j % 2) * D:(j % 2 + 1) * D],
                                                       a[q][:, k, j * P:j * P + st.rows], wc[:, k, :],
                                                       start=(k == 0), stop=(k == KC - 1))
                        ins.then_inc(s_mm[q], 1)

                    node_pass(pe, (0, product))

                @block.vector
                def _(dve):
                    v = nc.vector
                    dve.wait_ge(s_w, 48)
                    v.tensor_copy(b2b[:, :, :], b2c[:, :].rearrange("p (c a) -> p c a", a=1).broadcast_to([P, KC, P])
                                  ).then_inc(s_b2, 1)
                    dve.wait_ge(s_wp, 1)
                    v.tensor_copy(bc[:, :], bps[:, 0:D]).then_inc(s_b2, 1)
                    v.tensor_copy(wc[:, :, :], wps[:, :, :]).then_inc(s_wc, 1)
                    dve.wait_ge(s_b2, 2)

                    def scale(st):
                        q = st.par
                        dve.wait_ge(s_mm[q], done(st.use))
                        if not st.first:
                            dve.wait_ge(s_o[q], done(st.use - 1, 16))
                        rows = ps[q][0:st.rows, :, :].rearrange("p a b -> p (a b)")[:, 0:st.tiles * D]
                        b = bc[0:st.rows, :].rearrange("p (a d) -> p a d", a=1).broadcast_to([st.rows, st.tiles, D])
                        v.tensor_tensor(xw[q][0:st.rows, 0:st.tiles, :], rows.rearrange("p (a b) -> p a b", b=D), b,
                                        ALU.add).then_inc(s_sum[q], 1)
                        dve.wait_ge(s_sum[q], done(st.use))
                        for j in range(st.tiles):
                            ins = v.tensor_scalar(xw[q][0:st.rows, j, :], xw[q][0:st.rows, j, :],
                                                  dinv[0:st.rows, bass.ds(st.g * G + j, 1)], None, ALU.mult)
                        ins.then_inc(s_xw[q], 1)

                    node_pass(dve, (0, scale))

        def topk_table():
            with ExitStack() as c:
                p = Pass(c, "k")
                x, xw, agg = p.sb2("x", [P, G, D]), p.sb2("xw", [P, G, D]), p.sb2("agg", [P, G, D])
                x3, x3T = p.sb2("x3", [P, G, D]), p.sb2("x3T", [P, KC, GN])
                both = p.sb2("both", [P, G, 2 * D])
                work = p.sb("work", [P, G, D])
                vv, nmr = p.sb2("vv", [P, G, D]), p.sb2("nmr", [P, G])
                top8 = p.sb("top8", [P, G, 8])
                dg = p.sb2("dg", [P, G])
                sparse = p.sb2("sparse", [P, G, D])
                nidx = p.sb2("nidx", [P, G], I32)
                w = p.sb("w", [P, KC, 2 * D])
                ln, lmv, rstd = p.sb2("ln", [P, G, 6]), p.sb2("lmv", [P, G, 2]), p.sb2("rstd", [P, G])
                xps = p.ps2("xps", [P, KC, 512])
                ps = [p.ps(f"ps{j}", [P, 512]) for j in range(G)]
                s_w, s_wi, s_go = p.sem("s_w"), p.sem("s_wi"), p.sem("s_go")
                s_x, s_ni, s_agg, s_lv, s_var, s_sd, s_in, s_x3 = (
                    p.sem2("s_x"), p.sem2("s_ni"), p.sem2("s_agg"), p.sem2("s_lv"), p.sem2("s_var"), p.sem2("s_sd"),
                    p.sem2("s_in"), p.sem2("s_x3"))
                s_tr, s_xT = p.sem2("s_tr"), p.sem2("s_xT")
                s_u, s_dg, s_fac, s_t = p.sem2("s_u"), p.sem2("s_dg"), p.sem2("s_fac"), p.sem2("s_t")
                s_mm, s_bo = p.sem2("s_mm"), p.sem2("s_bo")
                s_k, s_sp = p.sem("s_k"), p.sem2("s_sp")
                s_o, s_so = p.sem2("s_o"), p.sem2("s_so")
                block = c.enter_context(nc.Block())

                @block.sync
                def _(sp):
                    sp.dma_start(w[:, :, 0:D], io["L3_gnn_W_self"].rearrange("(c p) n -> p c n", p=P)).then_inc(s_w, 16)
                    sp.dma_start(w[:, :, D:2 * D], io["L3_gnn_W_neigh"].rearrange("(c p) n -> p c n", p=P)).then_inc(s_w, 16)

                    def load(st):
                        q = st.par
                        if not st.first:
                            sp.wait_ge(s_in[q], done(st.use - 1))
                        sp.dma_start(x[q][0:st.rows, 0:st.tiles, :], nodes(x2d, st)).then_inc(s_x[q], 16)
                        sp.dma_start(xw[q][0:st.rows, 0:st.tiles, :], nodes(zd, st)).then_inc(s_x[q], 16)

                    node_pass(sp, (0, load))

                @block.gpsimd
                def _(pool):
                    pool.wait_ge(s_go, 1)

                    def gather(st):
                        gather_last(pool, st, agg, nidx, s_ni, s_agg, s_in)

                    def add_own(st):
                        q, r, t = st.par, st.rows, st.tiles
                        pool.wait_ge(s_x[q], done(st.use, 32))
                        pool.wait_ge(s_agg[q], agg_done(st))
                        nc.gpsimd.nop(nofuse=True)
                        nc.gpsimd.tensor_copy(dg[q][:, 0:t], dinv[:, bass.ds(st.g * G, t)]).then_inc(s_dg[q], 1)
                        nc.gpsimd.tensor_tensor(agg[q][0:r, 0:t, :], agg[q][0:r, 0:t, :], xw[q][0:r, 0:t, :],
                                                ALU.add).then_inc(s_t[q], 1)

                    def add_rest(st):
                        q, r, t = st.par, st.rows, st.tiles
                        pool.wait_ge(s_u[q], done(st.use))
                        if not st.first:
                            pool.wait_ge(s_x3[q], done(st.use - 1))
                        nc.gpsimd.nop(nofuse=True)
                        nc.gpsimd.tensor_tensor(vv[q][0:r, 0:t, :], agg[q][0:r, 0:t, :], x[q][0:r, 0:t, :],
                                                ALU.add).then_inc(s_in[q], 1)

                    node_pass(pool, (2, add_rest), (0, gather), (1, add_own))

                @block.vector
                def _(dve):
                    v = nc.vector
                    v.memset(top8[:, :, :], 0.0).then_inc(s_go, 1)
                    dve.wait_ge(s_w, 32)
                    for k in range(KC):
                        ins = v.tensor_tensor(w[:, k, k * P:(k + 1) * P], w[:, k, k * P:(k + 1) * P], ident[:, :], ALU.add)
                    ins.then_inc(s_wi, 1)
                    dve.wait_ge(s_go, 1)

                    def row_stats(st):
                        q, r, t = st.par, st.rows, st.tiles
                        dve.wait_ge(s_in[q], done(st.use))
                        for j in range(t):
                            ins = v.bn_stats(ln[q][0:r, j, :], vv[q][0:r, j, :])
                        ins.then_inc(s_lv[q], 1)
                        dve.wait_ge(s_lv[q], st.use * 2 + 1)
                        v.nop(nofuse=True)
                        for j in range(t):
                            ins = v.bn_aggr(lmv[q][0:r, j, :], ln[q][0:r, j, :])
                        ins.then_inc(s_var[q], 1)

                    def factors(st):
                        q, r, t = st.par, st.rows, st.tiles
                        dve.wait_ge(s_sd[q], done(st.use))
                        v.reciprocal(rstd[q][0:r, 0:t], rstd[q][0:r, 0:t]).then_inc(s_lv[q], 1)
                        dve.wait_ge(s_lv[q], st.use * 2 + 2)
                        v.scalar_tensor_tensor(nmr[q][0:r, 0:t], lmv[q][0:r, 0:t, 0], -1.0, rstd[q][0:r, 0:t],
                                               ALU.mult, ALU.mult).then_inc(s_fac[q], 1)

                    def select(st):
                        q, r, t = st.par, st.rows, st.tiles
                        per = 8 * G
                        base = st.g * per
                        dve.wait_ge(s_bo[q], st.use * G + t)
                        if not (isinstance(st.g, int) and st.g == 0):
                            dve.wait_ge(s_k, base)
                            dve.wait_ge(s_sp[1 - q], st.use if q == 0 else st.use + 1)
                        v.nop(nofuse=True)
                        at = 0
                        for u in range(TOPK // 8):
                            for j in range(t):
                                from_ = both[q][0:r, j, D:2 * D] if u == 0 else work[0:r, j, :]
                                if at >= t:
                                    dve.wait_ge(s_k, base + (at - t + 1))
                                    v.nop(nofuse=True)
                                v.max(top8[0:r, j, :], from_).then_inc(s_k, 1)
                                at += 1
                            for j in range(t):
                                from_ = both[q][0:r, j, D:2 * D] if u == 0 else work[0:r, j, :]
                                dve.wait_ge(s_k, base + (at - t + 1))
                                v.nop(nofuse=True)
                                v.match_replace(work[0:r, j, :], top8[0:r, j, :], from_, TAKEN).then_inc(s_k, 1)
                                at += 1
                        if not st.first:
                            dve.wait_ge(s_so[q], done(st.use - 1, 16))
                        dve.wait_ge(s_k, base + at)
                        v.scalar_tensor_tensor(sparse[q][0:r, 0:t, :], work[0:r, 0:t, :], TAKEN,
                                               both[q][0:r, 0:t, D:2 * D], ALU.is_equal, ALU.mult).then_inc(s_sp[q], 1)

                    node_pass(dve, (6, select), (3, factors), (2, row_stats))

                @block.tensor
                def _(pe):
                    pe.wait_ge(s_wi, 1)

                    def transpose(st):
                        q = st.par
                        pe.wait_ge(s_x3[q], done(st.use))
                        if not st.first:
                            pe.wait_ge(s_xT[q], done(st.use - 1))
                        for j in range(st.tiles):
                            for k in range(KC):
                                ins = nc.tensor.transpose(xps[q][:, k, j * P:j * P + st.rows],
                                                          x3[q][0:st.rows, j, k * P:(k + 1) * P],
                                                          ident[0:st.rows, 0:st.rows])
                        ins.then_inc(s_tr[q], 1)

                    def product(st):
                        q = st.par
                        pe.wait_ge(s_xT[q], done(st.use))
                        for j in range(st.tiles):
                            if not st.first or st.par == 1:
                                if st.par == 0:
                                    pe.wait_ge(s_bo[1], (st.use - 1) * G + (j + 1))
                                else:
                                    pe.wait_ge(s_bo[0], st.use * G + (j + 1))
                            for k in range(KC):
                                ins = nc.tensor.matmul(ps[j][0:st.rows, :], x3T[q][:, k, j * P:j * P + st.rows], w[:, k, :],
                                                       start=(k == 0), stop=(k == KC - 1))
                            ins.then_inc(s_mm[q], 1)

                    node_pass(pe, (5, product), (4, transpose))

                @block.scalar
                def _(act):
                    def deviation(st):
                        q = st.par
                        act.wait_ge(s_var[q], done(st.use))
                        nc.scalar.activation(rstd[q][0:st.rows, 0:st.tiles], lmv[q][0:st.rows, 0:st.tiles, 1], ACT.Sqrt,
                                             bias=eps_t[0:st.rows, 0:1]).then_inc(s_sd[q], 1)

                    def scale(st):
                        q, r, t = st.par, st.rows, st.tiles
                        act.wait_ge(s_t[q], done(st.use))
                        act.wait_ge(s_dg[q], done(st.use))
                        for j in range(t):
                            ins = nc.scalar.activation(agg[q][0:r, j, :], agg[q][0:r, j, :], ACT.Copy,
                                                       scale=dg[q][0:r, j:j + 1])
                        ins.then_inc(s_u[q], 1)

                    def normalise(st):
                        q, r, t = st.par, st.rows, st.tiles
                        act.wait_ge(s_fac[q], done(st.use))
                        if not st.first:
                            act.wait_ge(s_tr[q], done(st.use - 1))
                        for j in range(t):
                            ins = nc.scalar.activation(x3[q][0:r, j, :], vv[q][0:r, j, :], ACT.Identity,
                                                       bias=nmr[q][0:r, j:j + 1], scale=rstd[q][0:r, j:j + 1])
                        ins.then_inc(s_x3[q], 1)

                    def copy_T(st):
                        q = st.par
                        act.wait_ge(s_tr[q], done(st.use))
                        if not st.first:
                            act.wait_ge(s_mm[q], st.use * G)
                        nc.scalar.copy(x3T[q][:, :, 0:st.n], xps[q][:, :, 0:st.n]).then_inc(s_xT[q], 1)

                    def copy_out(st):
                        q = st.par
                        if not st.first:
                            act.wait_ge(s_o[q], done(st.use - 1, 16))
                            act.wait_ge(s_sp[q], done(st.use - 1))
                        for j in range(st.tiles):
                            act.wait_ge(s_mm[q], st.use * G + (j + 1))
                            nc.scalar.copy(both[q][0:st.rows, j, :], ps[j][0:st.rows, :]).then_inc(s_bo[q], 1)
                        act.wait_ge(s_bo[q], st.use * G + st.tiles)
                        act.dma_start(nodes(based, st), both[q][0:st.rows, 0:st.tiles, 0:D]).then_inc(s_o[q], 16)

                    def store(st):
                        q = st.par
                        act.wait_ge(s_sp[q], done(st.use))
                        act.dma_start(nodes(zd, st), sparse[q][0:st.rows, 0:st.tiles, :]).then_inc(s_so[q], 16)

                    node_pass(act, (5, copy_out), (7, store), (4, copy_T), (3, normalise), (2, deviation), (1, scale))
                    for q, uses in ((0, PAIRS + 1), (1, PAIRS)):
                        act.wait_ge(s_o[q], uses * 16)
                        act.wait_ge(s_so[q], uses * 16)

        def finish():
            with ExitStack() as c:
                p = Pass(c, "f")
                x, agg, y = p.sb2("x", [P, G, D]), p.sb2("agg", [P, G, D]), p.sb2("y", [P, G, D])
                nidx = p.sb2("nidx", [P, G], I32)
                vv, nmr = p.sb2("vv", [P, G, D]), p.sb2("nmr", [P, G])
                ln, lmv, rstd = p.sb2("ln", [P, G, 6]), p.sb2("lmv", [P, G, 2]), p.sb2("rstd", [P, G])
                s_fac, s_y = p.sem2("s_fac"), p.sem2("s_y")
                s_x, s_ni, s_agg, s_lv, s_var, s_sd, s_in, s_o = (
                    p.sem2("s_x"), p.sem2("s_ni"), p.sem2("s_agg"), p.sem2("s_lv"), p.sem2("s_var"), p.sem2("s_sd"),
                    p.sem2("s_in"), p.sem2("s_o"))
                block = c.enter_context(nc.Block())

                @block.sync
                def _(sp):
                    def load(st):
                        q = st.par
                        if not st.first:
                            sp.wait_ge(s_in[q], done(st.use - 1))
                        sp.dma_start(x[q][0:st.rows, 0:st.tiles, :], nodes(based, st)).then_inc(s_x[q], 16)

                    node_pass(sp, (0, load))

                @block.gpsimd
                def _(pool):
                    node_pass(pool, (0, lambda st: gather_last(pool, st, agg, nidx, s_ni, s_agg, s_in)))

                @block.vector
                def _(dve):
                    v = nc.vector

                    def combine(st):
                        q, r, t = st.par, st.rows, st.tiles
                        dve.wait_ge(s_x[q], done(st.use, 16))
                        dve.wait_ge(s_agg[q], agg_done(st))
                        if not st.first:
                            dve.wait_ge(s_y[q], done(st.use - 1))
                        for j in range(t):
                            ins = v.scalar_tensor_tensor(vv[q][0:r, j, :], agg[q][0:r, j, :],
                                                         rdeg[0:r, bass.ds(st.g * G + j, 1)], x[q][0:r, j, :],
                                                         ALU.mult, ALU.add)
                        ins.then_inc(s_in[q], 1)
                        dve.wait_ge(s_in[q], done(st.use))
                        for j in range(t):
                            ins = v.bn_stats(ln[q][0:r, j, :], vv[q][0:r, j, :])
                        ins.then_inc(s_lv[q], 1)
                        dve.wait_ge(s_lv[q], st.use * 2 + 1)
                        v.nop(nofuse=True)
                        for j in range(t):
                            ins = v.bn_aggr(lmv[q][0:r, j, :], ln[q][0:r, j, :])
                        ins.then_inc(s_var[q], 1)

                    def factors(st):
                        q, r, t = st.par, st.rows, st.tiles
                        dve.wait_ge(s_sd[q], done(st.use))
                        v.reciprocal(rstd[q][0:r, 0:t], rstd[q][0:r, 0:t]).then_inc(s_lv[q], 1)
                        dve.wait_ge(s_lv[q], st.use * 2 + 2)
                        v.scalar_tensor_tensor(nmr[q][0:r, 0:t], lmv[q][0:r, 0:t, 0], -1.0, rstd[q][0:r, 0:t],
                                               ALU.mult, ALU.mult).then_inc(s_fac[q], 1)

                    node_pass(dve, (1, factors), (0, combine))

                @block.scalar
                def _(act):
                    def deviation(st):
                        q = st.par
                        act.wait_ge(s_var[q], done(st.use))
                        nc.scalar.activation(rstd[q][0:st.rows, 0:st.tiles], lmv[q][0:st.rows, 0:st.tiles, 1], ACT.Sqrt,
                                             bias=eps_t[0:st.rows, 0:1]).then_inc(s_sd[q], 1)

                    def normalise(st):
                        q, r, t = st.par, st.rows, st.tiles
                        act.wait_ge(s_fac[q], done(st.use))
                        if not st.first:
                            act.wait_ge(s_o[q], done(st.use - 1, 16))
                        for j in range(t):
                            ins = nc.scalar.activation(y[q][0:r, j, :], vv[q][0:r, j, :], ACT.Identity,
                                                       bias=nmr[q][0:r, j:j + 1], scale=rstd[q][0:r, j:j + 1])
                        ins.then_inc(s_y[q], 1)
                        act.wait_ge(s_y[q], done(st.use))
                        act.dma_start(nodes(out, st), y[q][0:st.rows, 0:st.tiles, :]).then_inc(s_o[q], 16)

                    node_pass(act, (1, normalise), (0, deviation))
                    act.wait_ge(s_o[0], 16 * (PAIRS + 1))
                    act.wait_ge(s_o[1], 16 * PAIRS)

        with ExitStack() as c:
            s_e = signal("s_e")
            block = c.enter_context(nc.Block())

            @block.vector
            def _(dve):
                nc.vector.memset(eps_t[:, :], EPS).then_inc(s_e, 1)
                dve.wait_ge(s_e, 1)
        close_phase()

        edge_pass("e0", io["x"], "weight")
        close_phase()
        mlp_in("a", io["x"], False, io["L0_gnn_w1T"], io["L0_gnn_gamma1"], io["L0_gnn_beta1"], 0)
        close_phase()
        mlp0_out()
        close_phase()
        project()
        close_phase()
        attention()
        close_phase()
        edge_pass("e1", zd, "alpha")
        close_phase()
        mlp_in("d", x1d, True, io["L2_gnn_w1T"], io["L2_gnn_gamma"], io["L2_gnn_beta"], 2, bias=io["L2_gnn_b1"],
               store_rows=x2d)
        close_phase()
        gcn_table()
        close_phase()
        edge_pass("e2", zd, "plain")
        close_phase()
        topk_table()
        close_phase()
        edge_pass("e3", zd, "plain")
        close_phase()
        finish()
        close_phase()


_INS = ['x', 'src', 'dst', 'edge_weight', 'L0_gnn_w1T', 'L0_gnn_gamma1', 'L0_gnn_beta1', 'L0_gnn_w2T',
        'L0_gnn_eps_weight', 'L0_gnn_gamma_h', 'L0_gnn_beta_h', 'L1_gnn_W_flat', 'L1_gnn_a_src', 'L1_gnn_a_dst',
        'L2_gnn_w1T', 'L2_gnn_b1', 'L2_gnn_gamma', 'L2_gnn_beta', 'L2_gnn_w2', 'L2_gnn_b2', 'L2_gnn_w_gcnT',
        'L2_gnn_b_gcn', 'L3_gnn_W_self', 'L3_gnn_W_neigh']


def layout(inputs):
    a = dict(inputs)
    for name in ('L0_gnn_w1', 'L0_gnn_w2', 'L2_gnn_w1', 'L2_gnn_w_gcn'):
        a[name + 'T'] = a[name].transpose(1, 0)
    a['L1_gnn_W_flat'] = a['L1_gnn_W'].transpose(1, 0, 2).reshape(D, D)
    return {name: a[name] for name in _INS}


def kernel(**inputs):
    import numpy as _np
    import concourse.bacc as _bacc
    from concourse import mybir as _mybir
    from concourse.bass_utils import run_bass_kernel_spmd as _run

    nc = _bacc.Bacc("TRN2", target_bir_lowering=False, num_devices=1)
    arrays, args = {}, {}
    for name, a in layout(inputs).items():
        a = _np.ascontiguousarray(a)
        arrays[f"in_{name}_dram"] = a
        args[name] = nc.dram_tensor(f"in_{name}_dram", a.shape, _mybir.dt.from_np(a.dtype), kind="ExternalInput").ap()
    out = nc.dram_tensor("out_0_dram", (N, D), F32, kind="ExternalOutput").ap()
    build(nc, args, out)
    r = _run(nc, [arrays], core_ids=[0])
    return r.results[0]["out_0_dram"]
```
